# Optimizing a Trainium2 kernel written in Bass

```python
import numpy as np
import jax
import jax.numpy as jnp

def _softmax(x, axis=-1):
    return jax.nn.softmax(x, axis=axis)

def _gelu(x):
    return jax.nn.gelu(x, approximate=True)

def _silu(x):
    return jax.nn.silu(x)

def _sigmoid(x):
    return jax.nn.sigmoid(x)

def _layernorm(x, axis=-1, eps=1e-05):
    m = jnp.mean(x, axis=axis, keepdims=True)
    v = jnp.var(x, axis=axis, keepdims=True)
    return (x - m) / jnp.sqrt(v + eps)

def _scatter_add(tgt, idx, src, axis=0):
    return tgt.at[idx].add(src)

def _segment_sum(src, seg, n):
    return jax.ops.segment_sum(src, seg, n)
kernel_name = 'mk_audio_tower_d2_tok_audfeat1024_r4_413e8f'

def setup_inputs(seed: int=0):
    np.random.seed(seed)
    _w = jnp.asarray

    def _rec_inputs():
        import jax
        import jax.numpy as jnp
        _rk = jax.random.key(seed)
        x = -0.000125008 + 0.999885 * jax.random.normal(jax.random.fold_in(_rk, 1), (8, 128, 256), jnp.float32)
        return x
    x = _rec_inputs()

    def _L0_tok_setup():
        import jax, jax.numpy as jnp
        import numpy as np
        from jax import lax
        ALPHA = 0.1
        B, C_IN, T, D_MODEL = (32, 128, 512, 256)

        def _ewma_scan(xt):

            def step(carry, xi):
                carry = ALPHA * xi + (1.0 - ALPHA) * carry
                return (carry, carry)
            _, ys = lax.scan(step, xt[0], xt[1:])
            return jnp.concatenate([xt[:1], ys], axis=0)
        key = jax.random.key(seed)
        k_x, k_w, k_b = jax.random.split(key, 3)
        x = jax.random.normal(k_x, (B, C_IN, T), dtype=jnp.float32)
        bound = 1.0 / np.sqrt(C_IN)
        W = jax.random.uniform(k_w, (D_MODEL, C_IN), dtype=jnp.float32, minval=-bound, maxval=bound)
        b = jax.random.uniform(k_b, (D_MODEL,), dtype=jnp.float32, minval=-bound, maxval=bound)
        return {'x': x, 'W': W, 'b': b}
    _L0_tok_all = _L0_tok_setup()
    _L0_tok_in = {k: v for k, v in _L0_tok_all.items() if k in ('W', 'b')}
    del _L0_tok_all

    def _L0_attn_setup():
        import jax, jax.numpy as jnp
        import numpy as np
        DIM = 256
        N_HEADS = 16
        HEAD_DIM = DIM // N_HEADS
        key = jax.random.key(seed)
        ks = jax.random.split(key, 6)
        s = DIM ** (-0.5)
        return {'x': jax.random.normal(ks[0], (2, 512, DIM), dtype=jnp.float32), 'Wq': jax.random.normal(ks[1], (DIM, DIM), dtype=jnp.float32) * s, 'Wk': jax.random.normal(ks[2], (DIM, DIM), dtype=jnp.float32) * s, 'Wv': jax.random.normal(ks[3], (DIM, DIM), dtype=jnp.float32) * s, 'Wo': jax.random.normal(ks[4], (DIM, DIM), dtype=jnp.float32) * s, 'bo': jax.random.normal(ks[5], (DIM,), dtype=jnp.float32) * 0.01}
    _L0_attn_all = _L0_attn_setup()
    _L0_attn_in = {k: v for k, v in _L0_attn_all.items() if k in ('Wq', 'Wk', 'Wv', 'Wo', 'bo')}
    del _L0_attn_all

    def _L0_ffn_setup():
        import jax, jax.numpy as jnp
        import numpy as np
        D, H, O, E, TOPK = (256, 1024, 256, 8, 2)
        B, L = (2, 512)
        ROUTE_SCALE = 1.0
        key = jax.random.key(seed)
        ks = jax.random.split(key, 7)
        gb = float(np.sqrt(6.0 / (E + D)))
        return {'x': jax.random.normal(ks[0], (B, L, D), dtype=jnp.float32), 'gate_w': jax.random.uniform(ks[1], (E, D), jnp.float32, -gb, gb), 'gate_b': jnp.zeros((E,), jnp.float32), 'w1': jax.random.normal(ks[2], (E, D, H), jnp.float32) * 0.02, 'b1': jnp.zeros((E, H), jnp.float32), 'w2': jax.random.normal(ks[3], (E, H, O), jnp.float32) * 0.02, 'b2': jnp.zeros((E, O), jnp.float32)}
    _L0_ffn_all = _L0_ffn_setup()
    _L0_ffn_in = {k: v for k, v in _L0_ffn_all.items() if k in ('gate_w', 'gate_b', 'w1', 'b1', 'w2', 'b2')}
    del _L0_ffn_all

    def _L1_attn_setup():
        import jax, jax.numpy as jnp
        import numpy as np
        D_MODEL = 256
        N_HEADS = 16
        HEAD_DIM = D_MODEL // N_HEADS
        EPS = 1e-06

        def _split_heads(x):
            b, s, d = x.shape
            return x.reshape(b, s, N_HEADS, HEAD_DIM).transpose(0, 2, 1, 3)
        key = jax.random.key(seed)
        ks = jax.random.split(key, 10)
        s = 0.02
        return {'sequence': jax.random.normal(ks[0], (4, 512, D_MODEL), dtype=jnp.float32), 'ln_gamma': jnp.ones((D_MODEL,), jnp.float32), 'ln_beta': jnp.zeros((D_MODEL,), jnp.float32), 'Wq': jax.random.normal(ks[1], (D_MODEL, D_MODEL), jnp.float32) * s, 'bq': jnp.zeros((D_MODEL,), jnp.float32), 'Wk': jax.random.normal(ks[2], (D_MODEL, D_MODEL), jnp.float32) * s, 'bk': jnp.zeros((D_MODEL,), jnp.float32), 'Wv': jax.random.normal(ks[3], (D_MODEL, D_MODEL), jnp.float32) * s, 'bv': jnp.zeros((D_MODEL,), jnp.float32), 'Wo': jax.random.normal(ks[4], (D_MODEL, D_MODEL), jnp.float32) * s, 'bo': jnp.zeros((D_MODEL,), jnp.float32), 'mu': jnp.zeros((1, 1, 1, 1), jnp.float32)}
    _L1_attn_all = _L1_attn_setup()
    _L1_attn_in = {k: v for k, v in _L1_attn_all.items() if k in ('ln_gamma', 'ln_beta', 'Wq', 'bq', 'Wk', 'bk', 'Wv', 'bv', 'Wo', 'bo', 'mu')}
    del _L1_attn_all

    def _L1_ffn_setup():
        import jax, jax.numpy as jnp
        import numpy as np
        FP8_MAX = 448.0

        def quant_fp8(x):
            amax = jnp.max(jnp.abs(x)).astype(jnp.float32)
            scale = jnp.minimum(FP8_MAX / jnp.maximum(amax, 1e-12), FP8_MAX)
            x_fp8 = jnp.clip(x * scale, -FP8_MAX, FP8_MAX).astype(jnp.float8_e4m3fn)
            return (x_fp8, 1.0 / scale)
        key = jax.random.key(seed)
        k1, k2, k3 = jax.random.split(key, 3)
        B, S, IN, OUT = (4, 2048, 256, 256)
        input = jax.random.normal(k1, (B, S, IN), dtype=jnp.float32)
        bound = 1.0 / np.sqrt(IN)
        weight = jax.random.uniform(k2, (OUT, IN), dtype=jnp.float32, minval=-bound, maxval=bound)
        bias = jax.random.uniform(k3, (OUT,), dtype=jnp.float32, minval=-bound, maxval=bound)
        return {'input': input, 'weight': weight, 'bias': bias}
    _L1_ffn_all = _L1_ffn_setup()
    _L1_ffn_in = {k: v for k, v in _L1_ffn_all.items() if k in ('weight', 'bias')}
    del _L1_ffn_all
    return {'x': x, 'L0_tok_W': _L0_tok_in['W'], 'L0_tok_b': _L0_tok_in['b'], 'L0_attn_Wq': _L0_attn_in['Wq'], 'L0_attn_Wk': _L0_attn_in['Wk'], 'L0_attn_Wv': _L0_attn_in['Wv'], 'L0_attn_Wo': _L0_attn_in['Wo'], 'L0_attn_bo': _L0_attn_in['bo'], 'L0_ffn_gate_w': _L0_ffn_in['gate_w'], 'L0_ffn_gate_b': _L0_ffn_in['gate_b'], 'L0_ffn_w1': _L0_ffn_in['w1'], 'L0_ffn_b1': _L0_ffn_in['b1'], 'L0_ffn_w2': _L0_ffn_in['w2'], 'L0_ffn_b2': _L0_ffn_in['b2'], 'L1_attn_ln_gamma': _L1_attn_in['ln_gamma'], 'L1_attn_ln_beta': _L1_attn_in['ln_beta'], 'L1_attn_Wq': _L1_attn_in['Wq'], 'L1_attn_bq': _L1_attn_in['bq'], 'L1_attn_Wk': _L1_attn_in['Wk'], 'L1_attn_bk': _L1_attn_in['bk'], 'L1_attn_Wv': _L1_attn_in['Wv'], 'L1_attn_bv': _L1_attn_in['bv'], 'L1_attn_Wo': _L1_attn_in['Wo'], 'L1_attn_bo': _L1_attn_in['bo'], 'L1_attn_mu': _L1_attn_in['mu'], 'L1_ffn_weight': _L1_ffn_in['weight'], 'L1_ffn_bias': _L1_ffn_in['bias']}

def reference(x, L0_tok_W, L0_tok_b, L0_attn_Wq, L0_attn_Wk, L0_attn_Wv, L0_attn_Wo, L0_attn_bo, L0_ffn_gate_w, L0_ffn_gate_b, L0_ffn_w1, L0_ffn_b1, L0_ffn_w2, L0_ffn_b2, L1_attn_ln_gamma, L1_attn_ln_beta, L1_attn_Wq, L1_attn_bq, L1_attn_Wk, L1_attn_bk, L1_attn_Wv, L1_attn_bv, L1_attn_Wo, L1_attn_bo, L1_attn_mu, L1_ffn_weight, L1_ffn_bias):
    import jax
    import jax.numpy as jnp

    def _L0_tok_ref(x, W, b):
        import jax, jax.numpy as jnp
        import numpy as np
        from jax import lax
        ALPHA = 0.1
        B, C_IN, T, D_MODEL = (32, 128, 512, 256)

        def _ewma_scan(xt):

            def step(carry, xi):
                carry = ALPHA * xi + (1.0 - ALPHA) * carry
                return (carry, carry)
            _, ys = lax.scan(step, xt[0], xt[1:])
            return jnp.concatenate([xt[:1], ys], axis=0)
        xp = jnp.transpose(x, (0, 2, 1))
        xt = jnp.moveaxis(xp, 1, 0)
        fwd = _ewma_scan(xt)
        bwd = _ewma_scan(xt[::-1])[::-1]
        ewma = jnp.moveaxis((fwd + bwd) * 0.5, 0, 1)
        return jnp.einsum('btc,dc->btd', ewma, W) + b

    def _L0_attn_ref(x, Wq, Wk, Wv, Wo, bo):
        import jax, jax.numpy as jnp
        import numpy as np
        DIM = 256
        N_HEADS = 16
        HEAD_DIM = DIM // N_HEADS
        B, T, C = x.shape
        H, D = (N_HEADS, HEAD_DIM)
        q = (x @ Wq.T).reshape(B, T, H, D).transpose(0, 2, 1, 3)
        k = (x @ Wk.T).reshape(B, T, H, D).transpose(0, 2, 1, 3)
        v = (x @ Wv.T).reshape(B, T, H, D).transpose(0, 2, 1, 3)
        q = q * D ** (-0.5)
        attn = jnp.einsum('bhqd,bhkd->bhqk', q, k)
        causal_mask = jnp.triu(jnp.ones((T, T), dtype=bool), k=1)
        attn = jnp.where(causal_mask, -jnp.inf, attn)
        attn = jax.nn.softmax(attn, axis=-1)
        out = jnp.einsum('bhqk,bhkd->bhqd', attn, v)
        out = out.transpose(0, 2, 1, 3).reshape(B, T, C)
        return out @ Wo.T + bo

    def _L0_ffn_ref(x, gate_w, gate_b, w1, b1, w2, b2):
        import jax, jax.numpy as jnp
        import numpy as np
        D, H, O, E, TOPK = (256, 1024, 256, 8, 2)
        B, L = (2, 512)
        ROUTE_SCALE = 1.0
        Bb, Ll, Dd = x.shape
        N = Bb * Ll
        x_flat = x.reshape(N, Dd)
        logits = x_flat @ gate_w.T + gate_b
        probs = jax.nn.softmax(logits * ROUTE_SCALE, axis=-1)
        topk_vals, topk_idx = jax.lax.top_k(probs, TOPK)
        dense_gate = jnp.zeros((N, E), probs.dtype).at[jnp.arange(N)[:, None], topk_idx].set(topk_vals)
        h = jax.nn.relu(jnp.einsum('nd,edh->neh', x_flat, w1) + b1)
        y = jnp.einsum('neh,eho->neo', h, w2) + b2
        out_flat = jnp.einsum('ne,neo->no', dense_gate, y)
        return out_flat.reshape(Bb, Ll, O)

    def _L1_attn_ref(sequence, ln_gamma, ln_beta, Wq, bq, Wk, bk, Wv, bv, Wo, bo, mu):
        import jax, jax.numpy as jnp
        import numpy as np
        D_MODEL = 256
        N_HEADS = 16
        HEAD_DIM = D_MODEL // N_HEADS
        EPS = 1e-06

        def _split_heads(x):
            b, s, d = x.shape
            return x.reshape(b, s, N_HEADS, HEAD_DIM).transpose(0, 2, 1, 3)
        mean = jnp.mean(sequence, axis=-1, keepdims=True)
        var = jnp.mean(jnp.square(sequence - mean), axis=-1, keepdims=True)
        x = (sequence - mean) / jnp.sqrt(var + EPS) * ln_gamma + ln_beta
        q = _split_heads(x @ Wq.T + bq)
        k = _split_heads(x @ Wk.T + bk)
        v = _split_heads(x @ Wv.T + bv)
        scale = HEAD_DIM ** 0.5
        scores = jnp.einsum('bhqd,bhkd->bhqk', q, k) / scale
        scores = jax.nn.sigmoid(scores - mu) * jnp.exp(scores)
        scores = scores / jnp.sum(scores, axis=-1, keepdims=True)
        out = jnp.einsum('bhqk,bhkd->bhqd', scores, v)
        b, h, s, hd = out.shape
        out = out.transpose(0, 2, 1, 3).reshape(b, s, h * hd)
        return out @ Wo.T + bo

    def _L1_ffn_ref(input, weight, bias):
        import jax, jax.numpy as jnp
        import numpy as np
        FP8_MAX = 448.0

        def quant_fp8(x):
            amax = jnp.max(jnp.abs(x)).astype(jnp.float32)
            scale = jnp.minimum(FP8_MAX / jnp.maximum(amax, 1e-12), FP8_MAX)
            x_fp8 = jnp.clip(x * scale, -FP8_MAX, FP8_MAX).astype(jnp.float8_e4m3fn)
            return (x_fp8, 1.0 / scale)
        prev_shape = input.shape
        x2d = input.reshape(-1, weight.shape[1])
        w_fp8, w_scale = quant_fp8(weight)
        x_fp8, x_scale = quant_fp8(x2d)
        acc = jnp.matmul(x_fp8.astype(jnp.float32), w_fp8.astype(jnp.float32).T)
        out2d = (acc * (x_scale * w_scale) + bias).astype(jnp.bfloat16)
        out = out2d.reshape(*prev_shape[:-1], weight.shape[0]).astype(input.dtype)
        return out
    h = _L0_tok_ref(x, L0_tok_W, L0_tok_b)
    h = h + _L0_attn_ref(_layernorm(h, axis=-1), L0_attn_Wq, L0_attn_Wk, L0_attn_Wv, L0_attn_Wo, L0_attn_bo)
    h = h + _L0_ffn_ref(_layernorm(h, axis=-1), L0_ffn_gate_w, L0_ffn_gate_b, L0_ffn_w1, L0_ffn_b1, L0_ffn_w2, L0_ffn_b2)
    h = h + _L1_attn_ref(_layernorm(h, axis=-1), L1_attn_ln_gamma, L1_attn_ln_beta, L1_attn_Wq, L1_attn_bq, L1_attn_Wk, L1_attn_bk, L1_attn_Wv, L1_attn_bv, L1_attn_Wo, L1_attn_bo, L1_attn_mu)
    h = h + _L1_ffn_ref(_layernorm(h, axis=-1), L1_ffn_weight, L1_ffn_bias)
    return h

_drawn_inputs = setup_inputs


def setup_inputs(seed=0):
    import zlib

    import numpy as np

    out = dict(_drawn_inputs(seed))
    spreads = {'L0_ffn_gate_b': (0.0, 0.276),
     'L0_ffn_b1': (0.0, 0.1),
     'L0_ffn_b2': (0.0, 0.1),
     'L1_attn_ln_gamma': (1.0, 0.2),
     'L1_attn_ln_beta': (0.0, 0.383),
     'L1_attn_bq': (0.0, 0.8),
     'L1_attn_bk': (0.0, 0.8),
     'L1_attn_bv': (0.0, 0.1),
     'L1_attn_bo': (0.0, 0.1)}
    factors = {'L1_attn_Wq': 7.684, 'L1_attn_Wk': 7.139}
    for name, (base, spread) in spreads.items():
        noise = np.random.default_rng([zlib.crc32(name.encode()), seed]).standard_normal(out[name].shape)
        drawn = base * np.exp(spread * noise) if base else spread * noise
        out[name] = jnp.asarray(drawn.astype(out[name].dtype))
    for name, factor in factors.items():
        out[name] = (out[name] * factor).astype(out[name].dtype)
    return out
```

```python
from contextlib import ExitStack

import concourse.bass as bass
from concourse import mybir

F32 = mybir.dt.float32
BF16 = mybir.dt.bfloat16
I32 = mybir.dt.int32
U32 = mybir.dt.uint32
U8 = mybir.dt.uint8
ALU = mybir.AluOpType
ACT = mybir.ActivationFunctionType
AX = mybir.AxisListType.X

P = 128
B, C_IN, T = 8, 128, 256
D, HEADS = 256, 16
DH = D // HEADS
QT = T // P
TILES = B * QT
TOKENS = TILES * P
DC = D // P
EXPERTS, HID = 8, 1024
HC = HID // P
TOPK = 2
PAIRS = HEADS // 2
MOE_TILES = (TOKENS * TOPK + EXPERTS * (P - 1)) // P
SLOTS = MOE_TILES * P
LN_EPS = 1e-5
LN1_EPS = 1e-6
ALPHA = 0.1
NEG = -1e30
FP8_MAX = 448.0
CAP = TOKENS + P
ARENA = 159 * 1024
EXPERT_BYTES = 2 * HC * D * 4
EARLY = 3
Q_PARTS = (0, 0, 0, 1, 1, 2)
K_PARTS = (0, 1, 2, 0, 1, 0)
SLOTS6 = len(Q_PARTS)
ROWS = SLOTS6 * DH
SHIFT_ROW = ROWS


def wait(eng, sem, count):
    if not (isinstance(count, int) and count <= 0):
        eng.wait_ge(sem, count)


def stages(batch, first, last):
    return not isinstance(batch, int) or first <= batch <= last


def one(index):
    return bass.ds(index, 1)


def tower_kernel(nc, a, out):
    with ExitStack() as ctx:
        def sb(name, shape, dt):
            return ctx.enter_context(nc.sbuf_tensor(name, shape, dt))

        def sem(name):
            return ctx.enter_context(nc.semaphore(name))

        h = sb("h", [P, TILES, D], F32)
        ident = sb("ident", [P, P], F32)
        identb = sb("identb", [P, P], BF16)
        causal = sb("causal", [P, P], BF16)
        half_exp = sb("half_exp", [P, QT], F32)
        tok_wT = sb("tok_wT", [P, D], F32)
        w0T = sb("w0T", [P, 4, DC, D], F32)
        w1T = sb("w1T", [P, 4, DC, D], F32)
        fqT = sb("fqT", [P, DC, D], BF16)
        gate_wT = sb("gate_wT", [P, DC, EXPERTS], F32)
        tok_b = sb("tok_b", [P, D], F32)
        bo0 = sb("bo0", [P, D], F32)
        bv1 = sb("bv1", [P, D], F32)
        bo1 = sb("bo1", [P, D], F32)
        ffn_b = sb("ffn_b", [P, D], F32)
        cols = sb("cols", [P, 4, DC], F32)
        neg_mu = sb("neg_mu", [P, 1], F32)
        ones_row = sb("ones_row", [1, P], F32)
        onesb = sb("onesb", [P, P], BF16)
        before = sb("before", [P, P], BF16)
        iota8 = sb("iota8", [P, EXPERTS], F32)
        ones8 = sb("ones8", [P, EXPERTS], F32)
        iota_t = sb("iota_t", [1, MOE_TILES], F32)
        hot = sb("hot", [P, TOPK, TILES, EXPERTS], BF16)
        rank = sb("rank", [P, TOPK, TILES], F32)
        gates = sb("gates", [P, TILES, TOPK], F32)
        pos = sb("pos", [P, TOPK, TILES], I32)
        ypos = sb("ypos", [P, TOPK, QT], I32)
        run = sb("run", [P, EXPERTS], F32)
        g_l = sb("g_l", [P, QT, EXPERTS], F32)
        g_e = sb("g_e", [P, QT, EXPERTS], F32)
        g_p = sb("g_p", [P, QT, EXPERTS], F32)
        g_m = sb("g_m", [P, 3, QT], F32)
        top = sb("top", [P, QT, 8], F32)
        topi = sb("topi", [P, QT, 8], U32)
        topf = sb("topf", [P, TOPK, QT], F32)
        hot2 = sb("hot2", [P, TOPK, QT, EXPERTS], F32)
        hsum = sb("hsum", [P, QT, EXPERTS], BF16)
        rk = sb("rk", [P, QT, EXPERTS], F32)
        sel = sb("sel", [P, TOPK, QT, EXPERTS], F32)
        rk2 = sb("rk2", [P, TOPK, QT], F32)
        xslot = sb("xslot", [P, TOPK, QT], I32)
        pl = sb("pl", [P, 6, EXPERTS], F32)
        owner = sb("owner", [1, MOE_TILES, EXPERTS], F32)
        owned = sb("owned", [1, MOE_TILES, EXPERTS], F32)
        tile_w = sb("tile_w", [1, MOE_TILES], I32)
        tile_f = sb("tile_f", [1, MOE_TILES], F32)
        hot_base = sb("hot_base", [P, TILES, EXPERTS], F32)
        slot_base = sb("slot_base", [P, TILES], F32)
        pli = sb("pli", [P, EXPERTS], I32)
        cnt = sb("cnt", [1, EXPERTS], I32)
        tile_e = sb("tile_e", [1, MOE_TILES], I32)
        tile_row = sb("tile_row", [1, MOE_TILES], I32)
        gate_b = sb("gate_b", [P, EXPERTS], F32)
        mv = sb("mv", [P, 2, QT, 2], F32)
        bst = sb("bst", [P, 2, QT, 6], F32)
        veps = sb("veps", [P, 2, QT], F32)
        rstd = sb("rstd", [P, 2, QT], F32)
        arena = sb("arena", [P, ARENA], U8)

        used = [0]

        def carve(shape, dt, size):
            n = size
            for s in shape:
                n *= s
            start = used[0]
            used[0] = start + (n + 31) // 32 * 32
            assert used[0] <= ARENA, used[0]
            v = arena[:, start:start + n].bitcast(dt)
            if len(shape) == 2:
                v = v.rearrange("p (a b) -> p a b", a=shape[0])
            if len(shape) == 3:
                v = v.rearrange("p (a b c) -> p a b c", a=shape[0], b=shape[1])
            if len(shape) == 4:
                v = v.rearrange("p (a b c d) -> p a b c d", a=shape[0], b=shape[1], c=shape[2])
            return v

        ew_all = arena[:, 0:EXPERTS * EXPERT_BYTES].bitcast(F32).rearrange("p (e n) -> p e n", e=EXPERTS)
        w1s = ew_all[:, :, 0:DC * HID].rearrange("p e (c n) -> p e c n", c=DC)
        w2s = ew_all[:, :, DC * HID:].rearrange("p e (c n) -> p e c n", c=HC)

        used[0] = EXPERT_BYTES
        wraw = carve([9, DC, D], F32, 4)
        graw = carve([D], F32, 4)
        used[0] = EARLY * EXPERT_BYTES
        xin = carve([2, T], F32, 4)
        decay = carve([T], F32, 4)
        xs = carve([T], F32, 4)
        fw = carve([T], F32, 4)
        bw = carve([T], F32, 4)
        ew = carve([T], F32, 4)
        xh = carve([QT, D], F32, 4)
        x2h = carve([2, QT, D], F32, 4)
        xT = carve([DC, T], F32, 4)
        x2T = carve([DC, T], F32, 4)
        qkp = [carve([3, DC, T], BF16, 2) for _ in range(2)]
        qkr = [carve([DC, T], F32, 4) for _ in range(2)]
        stackq = carve([2, HEADS, T], BF16, 2)
        stackk = carve([2, HEADS, T], BF16, 2)
        vaug = carve([2, QT, HEADS, 32], F32, 4)
        mx = carve([HEADS, 3], F32, 4)
        mxn = carve([HEADS, 3], F32, 4)
        mneg = carve([QT, HEADS], BF16, 2)
        mT = carve([T], BF16, 2)
        probs = carve([PAIRS, 2, 512], F32, 4)
        oa = carve([4, T], F32, 4)
        rr = carve([QT, HEADS], F32, 4)
        onat = carve([QT, D], F32, 4)
        oT = carve([DC, T], F32, 4)

        used[0] = EXPERTS * EXPERT_BYTES
        xt_in = carve([2, D], F32, 4)
        xtT = carve([2, DC, P], F32, 4)
        hid = carve([HID], F32, 4)
        hidT = carve([2, HC, P], F32, 4)
        yt = carve([2, D], F32, 4)
        b2r = carve([EXPERTS, D], F32, 4)
        b1T = carve([HC, EXPERTS], F32, 4)
        b1raw = hid
        zeros = yt[:, 0, :]
        b1c = carve([2, HC], F32, 4)

        used[0] = 0
        first = carve([2, PAIRS, 2, 512], F32, 4)
        second = carve([4, 2, 512], F32, 4)
        stackq1 = carve([2, HEADS, T], BF16, 2)
        stackk1 = carve([2, HEADS, T], BF16, 2)
        n_y = w0T[:, 0:TOPK]
        n_xh = carve([QT, D], F32, 4)
        n_xT = carve([DC, T], F32, 4)
        n_qkp = [carve([3, DC, T], BF16, 2) for _ in range(2)]
        n_qkr = [carve([DC, T], F32, 4) for _ in range(2)]
        n_vaug = carve([2, QT, HEADS, 32], F32, 4)
        n_oa = carve([4, T], F32, 4)
        n_rr = carve([QT, HEADS], F32, 4)
        n_onat = carve([QT, D], F32, 4)
        n_oT = carve([DC, T], F32, 4)
        n_gate = carve([QT, TOPK], F32, 4)
        n_mom = carve([2, QT, 2], F32, 4)
        n_bst = carve([2, QT, 6], F32, 4)
        n_veps = carve([2, QT], F32, 4)
        n_rs = carve([2, QT], F32, 4)
        x3 = carve([TILES, D], F32, 4)
        amax = carve([2, QT], F32, 4)

        used[0] = 0
        w8 = carve([DC, D], F32, 4)
        amaxes = carve([2], F32, 4)
        amax_r = carve([2], F32, 4)
        scale_r = carve([4], F32, 4)
        scales = carve([4], F32, 4)
        f_y = carve([2, QT, D], F32, 4)
        f_e = carve([2, QT, D], I32, 4)
        f_t = carve([2, QT, D], F32, 4)
        f_q = carve([2, QT, D], BF16, 2)
        f_qT = carve([2, DC, T], BF16, 2)
        f_o = carve([2, QT, D], BF16, 2)
        f_out = carve([2, QT, D], F32, 4)

        psum = ctx.enter_context(nc.psum_tensor("psum", [P, 8, 512], F32))
        area = [psum[:, 0:2, :], psum[:, 2:4, :]]
        area3 = [*area, psum[:, 4:6, :]]
        pv_out = psum[:, 4:6, :].rearrange("p a (b t) -> p (a b) t", b=2)
        misc = [psum[:, 6, :], psum[:, 7, :]]

        turned = psum[:, 4:6, :]

        xg = nc.dram_tensor("xg", (EXPERTS * CAP, D), F32, kind="Internal").ap()
        yg = nc.dram_tensor("yg", (SLOTS, D), F32, kind="Internal").ap()
        scr = nc.dram_tensor("scr_parts", (2, 2, 3, D, T), BF16, kind="Internal").ap()

        names = """w_in settle consts ones_done wT_mm wT_done
            xs_done scans_done ew_done tok_mm h0_done stat1 mv1 veps1 rstd1 xh_done xT_mm xT_done
            q_mm k_mm v_mm qh_done kh_done v_done qr_done kr_done qm_done km_done ql_done kl_done
            scrq_w scrk_w stk_q stk_k sn_mm mxn_done mx_done mneg_done mT_mm mT_done mrow
            st_mm exp_done caus_done pv_mm oa_done ot1_mm rr_done on_done ot2_mm oT_done wo_mm
            hbo_done h1_done stat2 mv2 veps2 rstd2 xn_done xt2_mm xt2_done lg_mm gl_done ge_done g_step hsum_done rk_mm xslot_done
            w_exp p_step zfill w_late bias_done b_in b1_mm b1_done

            tx_mm xtT_done l1_mm hidA hidD th_mm reluA reluD l2_mm y_ev
            ypos_done comb_done n_mv n_eps n_rstd n_stat n_xh n_xT_mm n_xT_done n_q_mm n_k_mm n_v_mm
            n_qh n_kh n_qr n_kr n_qm n_km n_ql n_kl n_v_done n_scrq n_scrk n_stkq n_stkk set_done
            s1_mm f1_done s2_mm f2_done prodD prodP n_pv n_oa n_ot1 n_rr n_on n_ot2 n_oT n_wo n_hbo n_h3
            m_stat m_mv m_eps m_rstd x3_done am_done
            q_step w8_in am_mm am_row sc_mm qz_q fT_mm fT_done f_mm f_o f_out""".split()
        scat = [sem(f"scat{u}") for u in range(2)]
        x_ld = [sem(f"x_ld{u}") for u in range(2)]
        y_st = [sem(f"y_st{u}") for u in range(2)]
        o_out = [sem(f"o_out{u}") for u in range(2)]
        y_in = [sem(f"y_in{u}") for u in range(2)]
        S = {n: sem(n) for n in names}

        x_in = [sem(f"x_in{u}") for u in range(2)]

        LAST = B - 1

        def upto(eng, name, b, each=1):
            wait(eng, S[name], each * ((min(b, LAST) if isinstance(b, int) else b) + 1))

        def parity_count(k, u, d):
            return k + (u + d) // 2 + 1

        def dispatched(k, u, d):
            n = parity_count(k, u, d)
            return 16 + 16 * TOPK * QT * (max(n, 0) if isinstance(n, int) else n)

        def row(v):
            return v.rearrange("(o d) -> o d", o=1)

        def settled(eng):
            eng.sem_inc(S["settle"], 1)

        def batches(eng, iteration):
            for b in range(-2, 2):
                iteration(b, b % 2, b // 2)
            with eng.Fori(0, (B - 4) // 2) as it:
                for u in range(2):
                    iteration(it * 2 + (2 + u), u, it + 1)
            for b in range(B - 2, B + 2):
                iteration(b, b % 2, b // 2)

        with nc.Block() as block:
            @block.sync
            def _(sp):
                for i, name in enumerate(["L0_attn_Wq", "L0_attn_Wk", "L0_attn_Wv", "L0_attn_Wo", "L1_attn_Wq",
                                          "L1_attn_Wk", "L1_attn_Wv", "L1_attn_Wo"]):
                    sp.dma_start(wraw[:, i], a[name].rearrange("(j p) i -> p j i", p=P)).then_inc(S["w_in"], 16)
                sp.dma_start(wraw[:, 8, :, 0:C_IN],
                             a["L0_tok_W"].rearrange("(j p) i -> p j i", p=P)).then_inc(S["w_in"], 16)
                sp.dma_start(graw[0:EXPERTS, :], a["L0_ffn_gate_w"]).then_inc(S["w_in"], 16)
                for dst, name in ((tok_b, "L0_tok_b"), (bo0, "L0_attn_bo"), (bv1, "L1_attn_bv"),
                                  (bo1, "L1_attn_bo"), (ffn_b, "L1_ffn_bias")):
                    sp.dma_start(dst[:], row(a[name]).to_broadcast(list(dst.shape))).then_inc(S["w_in"], 16)
                with nc.allow_non_contiguous_dma(reason="256 scalars each, one per partition"):
                    for i, name in enumerate(["L1_attn_ln_gamma", "L1_attn_ln_beta", "L1_attn_bq", "L1_attn_bk"]):
                        sp.dma_start(cols[:, i, :], a[name].rearrange("(j p) -> p j", p=P)).then_inc(S["w_in"], 16)

                def load_expert(eng, e):
                    wait(eng, S["w_exp"], 32 * e)
                    eng.dma_start(w1s[:, e], a["L0_ffn_w1"][e].rearrange("(c p) n -> p c n", p=P)).then_inc(S["w_exp"], 16)
                    eng.dma_start(w2s[:, e], a["L0_ffn_w2"][e].rearrange("(c p) n -> p c n", p=P)).then_inc(S["w_exp"], 16)

                def load_x(b, u, k):
                    wait(sp, S["scans_done"], 2 * (b - 1))
                    sp.dma_start(xin[:, u, :], a["x"][one(b), :, :].rearrange("o c t -> c (o t)")).then_inc(x_in[u], 16)

                def bounce(b, u, which, done, landed_w, landed_r, stack):
                    sp.wait_ge(done, b + 1)
                    settled(sp)
                    wait(sp, S["st_mm"], PAIRS * (b - 1))
                    sp.dma_start(scr[u, which].rearrange("s (j p) t -> p (s j) t", p=P),
                                 qkp[which].rearrange("p s j t -> p (s j) t")).then_inc(landed_w, 16)

                def gather(b, u, which, landed_w, landed_r, stack):
                    sp.wait_ge(landed_w, 16 * (b + 1))
                    for i, part in enumerate((Q_PARTS, K_PARTS)[which]):
                        sp.dma_start(stack[DH * i:DH * (i + 1), u],
                                     scr[u, which, part].rearrange("(h d) t -> d h t", d=DH)).then_inc(landed_r, 16)

                def iteration(b, u, k):
                    if stages(b + 2, 0, LAST):
                        load_x(b + 2, u, k + 1)
                    if isinstance(b, int) and b == -1:
                        sp.wait_ge(S["wT_mm"], 10)
                    if isinstance(b, int) and stages(b + 2, 0, EARLY - 1):
                        load_expert(sp, b + 2)
                    if stages(b, 0, LAST):
                        sp.wait_ge(S["mT_done"], b + 1)
                        sp.dma_start(stackq[SHIFT_ROW:SHIFT_ROW + 1, u], mT[0:HEADS, :]).then_inc(S["mrow"], 16)
                    if stages(b + 1, 0, LAST):
                        v = 1 - u
                        bounce(b + 1, v, 0, S["ql_done"], S["scrq_w"], S["stk_q"], stackq)
                        bounce(b + 1, v, 1, S["kl_done"], S["scrk_w"], S["stk_k"], stackk)
                        gather(b + 1, v, 0, S["scrq_w"], S["stk_q"], stackq)
                        gather(b + 1, v, 1, S["scrk_w"], S["stk_k"], stackk)

                batches(sp, iteration)

            @block.gpsimd
            def _(pool):
                pool.dma_start(gate_b[:], row(a["L0_ffn_gate_b"]).to_broadcast([P, EXPERTS])).then_inc(scat[0], 16)
                pool.dma_start(neg_mu[:], a["L1_attn_mu"].rearrange("a b c d -> (a b) (c d)").to_broadcast([P, 1])).then_inc(scat[1], 16)
                pool.memset(ident[:], 0.0).then_inc(S["consts"], 1)
                pool.memset(identb[:], 0.0).then_inc(S["consts"], 1)
                pool.memset(causal[:], 0.0).then_inc(S["consts"], 1)
                pool.memset(half_exp[:], -0.5).then_inc(S["consts"], 1)
                pool.memset(before[:], 0.0).then_inc(S["consts"], 1)
                pool.memset(onesb[:], 1.0).then_inc(S["consts"], 1)
                pool.memset(ones_row[:], 1.0).then_inc(S["consts"], 1)
                pool.memset(ones8[:], 1.0).then_inc(S["consts"], 1)
                pool.memset(run[:], 0.0).then_inc(S["consts"], 1)
                pool.iota(iota8[:], pattern=[[1, EXPERTS]], base=0, channel_multiplier=0,
                          allow_small_or_imprecise_dtypes=True).then_inc(S["consts"], 1)
                pool.iota(iota_t[:], pattern=[[1, MOE_TILES]], base=0, channel_multiplier=0,
                          allow_small_or_imprecise_dtypes=True).then_inc(S["consts"], 1)
                pool.wait_ge(S["consts"], 11)
                pool.affine_select(out=before[:], in_=before[:], compare_op=ALU.is_ge, fill=1.0, base=0,
                                   pattern=[[-1, P]], channel_multiplier=1).then_inc(S["consts"], 1)
                for m in (ident, identb):
                    pool.affine_select(out=m[:], in_=m[:], compare_op=ALU.not_equal, fill=1.0, base=0,
                                       pattern=[[-1, P]], channel_multiplier=1).then_inc(S["consts"], 1)
                pool.affine_select(out=causal[:], in_=causal[:], compare_op=ALU.is_ge, fill=NEG, base=0,
                                   pattern=[[-1, P]], channel_multiplier=1).then_inc(S["consts"], 1)

                def norm_scale(b, n, got, s_eps, s_rstd):
                    pool.wait_ge(got, QT * (b + 1))
                    settled(pool)
                    pool.tensor_scalar(veps[:, n, :], mv[:, n, :, 1], LN_EPS, None, ALU.add).then_inc(s_eps, 1)
                    pool.wait_ge(s_eps, b + 1)
                    pool.tensor_tensor(rstd[:, n, :], veps[:, n, :], half_exp[:], ALU.pow).then_inc(s_rstd, 1)

                def causal_probs(b, p):
                    pool.wait_ge(S["exp_done"], PAIRS * b + p + 1)
                    settled(pool)
                    v = probs[:, p].rearrange("p i (n q) -> p (i n) q", q=P)[:, 0:8:2, :]
                    pool.affine_select(out=v, in_=v, compare_op=ALU.is_ge, fill=0.0, base=0,
                                       pattern=[[0, 4], [1, P]], channel_multiplier=-1).then_inc(S["caus_done"], 1)

                def iteration(b, u, k):
                    if stages(b - 1, 0, LAST):
                        pool.wait_ge(S["xh_done"], QT * b)
                        v = h[:, bass.ds((b - 1) * QT, QT), :]
                        pool.tensor_tensor(v, v, bo0[:].rearrange("p (o d) -> p o d", o=1).to_broadcast([P, QT, D]),
                                           ALU.add).then_inc(S["hbo_done"], 1)
                    for p in range(PAIRS):
                        if stages(b, 0, LAST):
                            causal_probs(b, p)
                        if p == 4 and stages(b + 2, 0, LAST):
                            norm_scale(b + 2, 0, S["mv1"], S["veps1"], S["rstd1"])
                    if stages(b - 1, 0, LAST):
                        norm_scale(b - 1, 1, S["mv2"], S["veps2"], S["rstd2"])
                    if stages(b - 2, 0, LAST):
                        pool.wait_ge(S["xslot_done"], b)
                        settled(pool)
                        for c in range(TOPK):
                            for q in range(QT):
                                pool.indirect_dma_start(
                                    out=xg, out_offset=bass.IndirectOffsetOnAxis(ap=xslot[:, c, q:q + 1], axis=0),
                                    in_=x2h[:, u, q, :], in_offset=None).then_inc(scat[u], 16)

                batches(pool, iteration)
                for u in range(2):
                    pool.wait_ge(scat[u], 16 + 16 * TOPK * QT * B // 2)

            @block.scalar
            def _(act):
                for n in range(8):
                    act.wait_ge(S["wT_mm"], n + 1)
                    w = (w0T, w1T)[n // 4][:, n % 4].rearrange("p c d -> p (c d)")
                    act.activation(w, misc[n % 2], ACT.Copy, scale=DH ** -0.5 if n % 4 == 0 else 1.0).then_inc(S["wT_done"], 1)
                act.wait_ge(S["wT_mm"], 9)
                act.activation(tok_wT[:], misc[0][:, 0:D], ACT.Copy, scale=0.5).then_inc(S["wT_done"], 1)
                act.wait_ge(S["wT_mm"], 10)
                act.copy(gate_wT[:].rearrange("p c e -> p (c e)"), misc[1][:, 0:DC * EXPERTS]).then_inc(S["wT_done"], 1)
                act.mul(cols[:, 2, :], cols[:, 2, :], DH ** -0.5).then_inc(S["wT_done"], 1)
                act.wait_ge(scat[1], 16)
                act.mul(neg_mu[:], neg_mu[:], -1.0).then_inc(S["wT_done"], 1)

                def iteration(b, u, k):
                    v = 1 - u
                    if stages(b + 1, 0, LAST):
                        act.wait_ge(S["xT_mm"], b + 2)
                        wait(act, S["v_mm"], b + 1)
                        act.copy(xT.rearrange("p c t -> p (c t)"), misc[1]).then_inc(S["xT_done"], 1)
                    if stages(b - 2, 0, LAST):
                        act.wait_ge(S["xt2_mm"], b - 1)
                        act.copy(x2T.rearrange("p c t -> p (c t)"), misc[0]).then_inc(S["xt2_done"], 1)
                    if stages(b, 0, LAST):
                        act.wait_ge(S["mT_mm"], b + 1)
                        wait(act, S["mrow"], 16 * b)
                        act.copy(mT[0:HEADS, :], misc[0].bitcast(BF16)[0:HEADS, 0:T]).then_inc(S["mT_done"], 1)
                    if stages(b + 1, 0, LAST):
                        act.wait_ge(S["q_mm"], b + 2)
                        wait(act, S["scrq_w"], 16 * (b + 1))
                        act.activation(qkp[0][:, 0].rearrange("p c t -> p (c t)"), misc[0], ACT.Copy,
                                       scale=1.0).then_inc(S["qh_done"], 1)
                        act.wait_ge(S["k_mm"], b + 2)
                        wait(act, S["scrk_w"], 16 * (b + 1))
                        act.copy(qkp[1][:, 0].rearrange("p c t -> p (c t)"), misc[1]).then_inc(S["kh_done"], 1)
                    if stages(b - 2, 0, LAST):
                        act.wait_ge(S["gl_done"], b - 1)
                        act.activation(g_e[:], g_l[:], ACT.Exp).then_inc(S["ge_done"], 1)
                    if stages(b + 1, 0, LAST):
                        act.wait_ge(S["v_mm"], b + 2)
                        wait(act, S["pv_mm"], 4 * b)
                        act.copy(vaug[:, v, :, :, 0:DH],
                                 turned[:, 0, :].rearrange("p (q h d) -> p q h d", q=QT, h=HEADS)).then_inc(S["v_done"], 1)
                        act.wait_ge(S["qr_done"], b + 2)
                        act.copy(qkp[0][:, 1], qkr[0]).then_inc(S["qm_done"], 1)
                        act.wait_ge(S["kr_done"], b + 2)
                        act.copy(qkp[1][:, 1], qkr[1]).then_inc(S["km_done"], 1)
                    if stages(b - 1, 0, LAST):
                        act.wait_ge(S["ot2_mm"], b)
                        wait(act, S["wo_mm"], b - 1)
                        act.copy(oT.rearrange("p c t -> p (c t)"), turned[:, 1, :]).then_inc(S["oT_done"], 1)
                    for p in range(PAIRS):
                        if stages(b, 0, LAST):
                            act.wait_ge(S["st_mm"], PAIRS * b + p + 1)
                            wait(act, S["pv_mm"], 4 * (b - 1) + p // 2 + 1)
                            act.activation(probs[:, p, :, 0:384], area[p % 2][:, :, 0:384], ACT.Exp).then_inc(S["exp_done"], 1)
                    if stages(b, 0, LAST):
                        act.wait_ge(S["pv_mm"], 4 * (b + 1))
                        wait(act, S["ot1_mm"], b)
                        act.copy(oa, pv_out).then_inc(S["oa_done"], 1)

                batches(act, iteration)

            @block.vector
            def _(dve):
                dve.memset(decay, 1.0 - ALPHA).then_inc(S["ones_done"], 1)
                dve.memset(vaug[:, :, :, :, DH:32], 1.0).then_inc(S["ones_done"], 1)
                dve.memset(xslot[:], 0).then_inc(S["xslot_done"], 1)
                dve.memset(stackk[SHIFT_ROW:SHIFT_ROW + 1], 1.0).then_inc(S["ones_done"], 1)
                dve.wait_ge(S["ones_done"], 3)

                def split_rest(b, which, scale, first, rest):
                    dve.wait_ge(first, b + 1)
                    dve.scalar_tensor_tensor(out=qkr[which], in0=misc[which].rearrange("p (c t) -> p c t", c=DC),
                                             scalar=scale, in1=qkp[which][:, 0], op0=ALU.mult,
                                             op1=ALU.subtract).then_inc(rest, 1)

                def split_last(b, which, second, last):
                    dve.wait_ge(second, b + 1)
                    dve.tensor_tensor(qkp[which][:, 2], qkr[which], qkp[which][:, 1], ALU.subtract).then_inc(last, 1)

                def statistics(b, n, s_stat, s_mv):
                    settled(dve)
                    for q in range(QT):
                        dve.bn_stats(bst[:, n, q, :], h[:, one(b * QT + q), :].rearrange("p o d -> p (o d)")).then_inc(s_stat, 1)
                    dve.wait_ge(s_stat, QT * (b + 1))
                    settled(dve)
                    for q in range(QT):
                        dve.bn_aggr(mv[:, n, q, :], bst[:, n, q, :]).then_inc(s_mv, 1)

                def normalise(b, n, dst, s_rstd, s_out):
                    dve.wait_ge(s_rstd, b + 1)
                    for q in range(QT):
                        dve.tensor_scalar(dst(q), h[:, one(b * QT + q), :], mv[:, n, q, 0:1], rstd[:, n, q:q + 1],
                                          ALU.subtract, ALU.mult).then_inc(s_out, 1)

                GATE_STEPS = 16
                step = [0]

                def link(g, ins):
                    step[0] += 1
                    ins.then_inc(S["g_step"], 1)
                    dve.wait_ge(S["g_step"], g * GATE_STEPS + step[0])

                def over(v, axis, shape):
                    v = v.rearrange("p (o e) -> p o e", o=1) if axis == 1 else v.rearrange("p (q o) -> p q o", o=1)
                    return v.to_broadcast(shape)

                def gate_logits(g):
                    QE = [P, QT, EXPERTS]
                    step[0] = 0
                    dve.wait_ge(S["lg_mm"], g + 1)
                    if isinstance(g, int) and g == 0:
                        dve.wait_ge(scat[0], 16)
                    ins = dve.tensor_tensor(g_l[:], misc[1][:, 0:QT * EXPERTS].rearrange("p (q e) -> p q e", q=QT),
                                            over(gate_b[:], 1, QE), ALU.add)
                    link(g, ins)
                    link(g, dve.tensor_reduce(g_m[:, 0, :], g_l[:], AX, ALU.max))
                    dve.tensor_tensor(g_l[:], g_l[:], over(g_m[:, 0, :], 2, QE), ALU.subtract).then_inc(S["gl_done"], 1)

                def choose_experts(g):
                    QE = [P, QT, EXPERTS]
                    dve.wait_ge(S["ge_done"], g + 1)
                    link(g, dve.tensor_reduce(g_m[:, 1, :], g_e[:], AX, ALU.add))
                    link(g, dve.reciprocal(g_m[:, 2, :], g_m[:, 1, :]))
                    link(g, dve.tensor_tensor(g_p[:], g_e[:], over(g_m[:, 2, :], 2, QE), ALU.mult))
                    settled(dve)
                    for q in range(QT):
                        ins = dve.max(top[:, q, :], g_p[:, q, :])
                    link(g, ins)
                    settled(dve)
                    for q in range(QT):
                        ins = dve.max_index(topi[:, q, :], top[:, q, :], g_p[:, q, :])
                    link(g, ins)
                    dve.tensor_copy(gates[:, bass.ds(g * QT, QT), :], top[:, :, 0:TOPK])
                    link(g, dve.tensor_copy(topf[:], topi[:, :, 0:TOPK].rearrange("p q c -> p c q")))
                    for c in range(TOPK):
                        link(g, dve.tensor_tensor(hot2[:, c], over(iota8[:], 1, QE), over(topf[:, c, :], 2, QE), ALU.is_equal))
                    dve.tensor_tensor(hsum[:], hot2[:, 0], hot2[:, 1], ALU.add).then_inc(S["hsum_done"], 1)
                    link(g, dve.tensor_copy(hot[:, :, bass.ds(g * QT, QT), :], hot2[:]))

                def rank_tokens(g, u, before_it):
                    QE = [P, QT, EXPERTS]
                    dve.wait_ge(S["rk_mm"], g + 1)
                    m = misc[0][:, 0:3 * EXPERTS].rearrange("p (q e) -> p q e", e=EXPERTS)
                    link(g, dve.tensor_tensor(rk[:], m[:, 0:QT, :], over(run[:], 1, QE), ALU.add))
                    link(g, dve.tensor_tensor(run[:], m[:, 2, :], run[:], ALU.add))
                    for c in range(TOPK):
                        link(g, dve.tensor_tensor(sel[:, c], hot2[:, c], rk[:], ALU.mult))
                    link(g, dve.tensor_reduce(rk2[:], sel[:], AX, ALU.add))
                    dve.tensor_copy(rank[:, :, bass.ds(g * QT, QT)], rk2[:])
                    dve.wait_ge(scat[1 - u], before_it)
                    dve.scalar_tensor_tensor(out=xslot[:], in0=topf[:], scalar=float(CAP), in1=rk2[:], op0=ALU.mult,
                                             op1=ALU.add).then_inc(S["xslot_done"], 1)
                    assert step[0] == GATE_STEPS, step[0]

                def iteration(b, u, k):
                    if stages(b, 0, LAST):
                        wait(dve, S["mneg_done"], 2 * b)
                        for p in range(PAIRS):
                            dve.wait_ge(S["sn_mm"], PAIRS * b + p + 1)
                            dve.tensor_reduce(mx[:, 2 * p:2 * p + 2, :],
                                              area3[p % 3][:, :, 0:3 * P].rearrange("p i (n k) -> p i n k", k=P),
                                              AX, ALU.max).then_inc(S["mx_done"], 1)
                        dve.wait_ge(S["mx_done"], PAIRS * (b + 1))
                        dve.tensor_scalar(mxn, mx, -1.0, None, ALU.mult).then_inc(S["mxn_done"], 1)
                        dve.wait_ge(S["mxn_done"], b + 1)
                        wait(dve, S["mT_mm"], b)
                        dve.tensor_copy(mneg[:, 0, :], mxn[:, :, 2]).then_inc(S["mneg_done"], 1)
                        dve.tensor_tensor(mneg[:, 1, :], mxn[:, :, 0], mxn[:, :, 1], ALU.min).then_inc(S["mneg_done"], 1)
                    if stages(b + 2, 0, LAST):
                        dve.wait_ge(x_in[u], 16 * (k + 2))
                        wait(dve, S["scans_done"], 2 * (b + 2))
                        x = xin[:, u, :]
                        dve.tensor_scalar(xs, x, ALPHA, None, ALU.mult).then_inc(S["xs_done"], 1)
                        dve.wait_ge(S["xs_done"], b + 3)
                        wait(dve, S["ew_done"], b + 2)
                        dve.tensor_tensor_scan(fw, decay, xs, x[:, 0:1], ALU.mult, ALU.add).then_inc(S["scans_done"], 1)
                        dve.tensor_tensor_scan(bw[:, ::-1], decay, xs[:, ::-1], x[:, T - 1:T], ALU.mult,
                                               ALU.add).then_inc(S["scans_done"], 1)
                        dve.wait_ge(S["scans_done"], 2 * (b + 3))
                        wait(dve, S["tok_mm"], b + 2)
                        dve.tensor_tensor(ew, fw, bw, ALU.add).then_inc(S["ew_done"], 1)
                    if stages(b - 2, 0, LAST):
                        gate_logits(b - 2)
                    if stages(b - 1, 0, LAST):
                        dve.wait_ge(S["ot1_mm"], b)
                        wait(dve, S["ot2_mm"], b - 1)
                        wait(dve, S["on_done"], QT * (b - 1))
                        o1 = turned.rearrange("p q (h c) -> p q h c", c=32)
                        for q in range(QT):
                            dve.reciprocal(rr[:, q, :], o1[:, q, :, DH]).then_inc(S["rr_done"], 1)
                        for q in range(QT):
                            dve.wait_ge(S["rr_done"], QT * (b - 1) + q + 1)
                            dve.tensor_tensor(onat[:, q].rearrange("p (h d) -> p h d", d=DH), o1[:, q, :, 0:DH],
                                              rr[:, q, :].rearrange("p (h o) -> p h o", o=1).to_broadcast([P, HEADS, DH]),
                                              ALU.mult).then_inc(S["on_done"], 1)
                    if stages(b + 1, 0, LAST):
                        wait(dve, S["km_done"], b + 1)
                        wait(dve, S["kl_done"], b + 1)
                        split_rest(b + 1, 0, 1.0, S["qh_done"], S["qr_done"])
                        split_rest(b + 1, 1, 1.0, S["kh_done"], S["kr_done"])
                        split_last(b + 1, 0, S["qm_done"], S["ql_done"])
                        split_last(b + 1, 1, S["km_done"], S["kl_done"])
                    if stages(b + 2, 0, LAST):
                        dve.wait_ge(S["tok_mm"], b + 3)
                        v = h[:, bass.ds((b + 2) * QT, QT), :]
                        dve.tensor_tensor(v, misc[0].rearrange("p (q d) -> p q d", q=QT),
                                          tok_b[:].rearrange("p (o d) -> p o d", o=1).to_broadcast([P, QT, D]),
                                          ALU.add).then_inc(S["h0_done"], 1)
                        dve.wait_ge(S["h0_done"], b + 3)
                        wait(dve, S["xh_done"], QT * (b + 2))
                        statistics(b + 2, 0, S["stat1"], S["mv1"])
                    if stages(b - 2, 0, LAST):
                        choose_experts(b - 2)
                    if stages(b + 2, 0, LAST):
                        wait(dve, S["xT_mm"], b + 2)
                        normalise(b + 2, 0, lambda q: xh[:, q:q + 1, :], S["rstd1"], S["xh_done"])
                    if stages(b - 1, 0, LAST):
                        dve.wait_ge(S["wo_mm"], b)
                        dve.wait_ge(S["hbo_done"], b)
                        v = h[:, bass.ds((b - 1) * QT, QT), :]
                        dve.tensor_tensor(v, misc[1].rearrange("p (q d) -> p q d", q=QT), v, ALU.add).then_inc(S["h1_done"], 1)
                        dve.wait_ge(S["h1_done"], b)
                        wait(dve, S["xn_done"], QT * (b - 1))
                        statistics(b - 1, 1, S["stat2"], S["mv2"])
                    if stages(b - 2, 0, LAST):
                        rank_tokens(b - 2, u, dispatched(k, u, -3))
                    if stages(b - 1, 0, LAST):
                        dve.wait_ge(scat[1 - u], dispatched(k, u, -3))
                        normalise(b - 1, 1, lambda q: x2h[:, 1 - u, q:q + 1, :], S["rstd2"], S["xn_done"])

                batches(dve, iteration)

                steps = [0]

                def chain(ins):
                    steps[0] += 1
                    ins.then_inc(S["p_step"], 1)
                    dve.wait_ge(S["p_step"], steps[0])

                padded, tiles, end, start, base, offset = (pl[:, i, :] for i in range(6))
                chain(dve.tensor_scalar(pli[:], run[:], float(P - 1), None, ALU.add))
                chain(dve.tensor_single_scalar(pli[:], pli[:], P.bit_length() - 1, op=ALU.arith_shift_right))
                chain(dve.tensor_copy(tiles, pli[:]))
                chain(dve.tensor_tensor_scan(end, ones8[:], tiles, 0.0, ALU.mult, ALU.add))
                chain(dve.tensor_tensor(start, end, tiles, ALU.subtract))
                chain(dve.tensor_scalar(base, start, float(P), None, ALU.mult))
                chain(dve.scalar_tensor_tensor(out=offset, in0=iota8[:], scalar=float(CAP), in1=base, op0=ALU.mult,
                                               op1=ALU.subtract))
                chain(dve.tensor_copy(cnt[:], run[0:1, :]))
                ME = [1, MOE_TILES, EXPERTS]
                chain(dve.tensor_tensor(owner[:], over(iota_t[:], 2, ME), over(start[0:1], 1, ME), ALU.is_ge))
                chain(dve.tensor_tensor(owned[:], over(iota_t[:], 2, ME), over(end[0:1], 1, ME), ALU.is_lt))
                chain(dve.tensor_tensor(owner[:], owner[:], owned[:], ALU.mult))
                chain(dve.tensor_tensor(owned[:], owner[:], over(iota8[0:1, :], 1, ME), ALU.mult))
                chain(dve.tensor_reduce(tile_f[:], owned[:], AX, ALU.add))
                chain(dve.tensor_copy(tile_e[:], tile_f[:]))
                chain(dve.tensor_scalar(tile_f[:], tile_f[:], 32.0, 16.0 + 32.0 * (1 - EARLY), ALU.mult, ALU.add))
                chain(dve.tensor_scalar(tile_w[:], tile_f[:], 16.0, None, ALU.max))
                chain(dve.tensor_scalar(iota_t[:], iota_t[:], float(P), None, ALU.mult))
                chain(dve.tensor_tensor(owned[:], over(iota_t[:], 2, ME), over(offset[0:1], 1, ME), ALU.add))
                chain(dve.tensor_tensor(owned[:], owned[:], owner[:], ALU.mult))
                chain(dve.tensor_reduce(tile_f[:], owned[:], AX, ALU.add))
                chain(dve.tensor_copy(tile_row[:], tile_f[:]))
                for c in range(TOPK):
                    chain(dve.tensor_tensor(hot_base[:], hot[:, c], over(base, 1, [P, TILES, EXPERTS]), ALU.mult))
                    chain(dve.tensor_reduce(slot_base[:], hot_base[:], AX, ALU.add))
                    chain(dve.tensor_tensor(pos[:, c, :], rank[:, c, :], slot_base[:], ALU.add))

            @block.tensor
            def _(pe):
                pe.wait_ge(S["w_in"], 19 * 16)
                pe.wait_ge(S["consts"], 15)
                for n in range(8):
                    if n >= 2:
                        pe.wait_ge(S["wT_done"], n - 1)
                    for c in range(DC):
                        for j in range(DC):
                            mm = pe.transpose(misc[n % 2][:, c * D + j * P:c * D + (j + 1) * P],
                                              wraw[:, n, j, c * P:(c + 1) * P], ident[:])
                    mm.then_inc(S["wT_mm"], 1)
                pe.wait_ge(S["wT_done"], 7)
                for j in range(DC):
                    mm = pe.transpose(misc[0][:, j * P:(j + 1) * P], wraw[:, 8, j, 0:P], ident[:])
                mm.then_inc(S["wT_mm"], 1)
                pe.wait_ge(S["wT_done"], 8)
                for c in range(DC):
                    mm = pe.transpose(misc[1][:, c * EXPERTS:(c + 1) * EXPERTS], graw[0:EXPERTS, c * P:(c + 1) * P],
                                      ident[0:EXPERTS, 0:EXPERTS])
                mm.then_inc(S["wT_mm"], 1)
                pe.wait_ge(S["wT_done"], 12)
                pe.wait_ge(S["ones_done"], 3)

                def turn(bank, src, done):
                    for c in range(DC):
                        for q in range(QT):
                            mm = pe.transpose(bank[:, c * T + q * P:c * T + (q + 1) * P], src(q, c), ident[:])
                    mm.then_inc(done, 1)

                def project_rows(bank, w, done):
                    for j in range(DC):
                        for c in range(DC):
                            mm = pe.matmul(bank[:, j * T:(j + 1) * T], w0T[:, w, c, j * P:(j + 1) * P], xT[:, c, :],
                                           start=(c == 0), stop=(c == DC - 1))
                    mm.then_inc(done, 1)

                def project_tokens(bank, x, w, done):
                    for q in range(QT):
                        for c in range(DC):
                            mm = pe.matmul(bank[:, q * D:(q + 1) * D], x[:, c, q * P:(q + 1) * P], w(c),
                                           start=(c == 0), stop=(c == DC - 1))
                    mm.then_inc(done, 1)

                def scores_for_max(b, u):
                    pe.wait_ge(S["stk_q"], 16 * SLOTS6 * (b + 1))
                    pe.wait_ge(S["stk_k"], 16 * SLOTS6 * (b + 1))
                    for p in range(PAIRS):
                        if p < 2:
                            wait(pe, S["exp_done"], PAIRS * b - 1 + p)
                        elif p == 2:
                            wait(pe, S["oa_done"], b)
                        else:
                            pe.wait_ge(S["mx_done"], PAIRS * b + p - 2)
                        for i in range(2):
                            hd = 2 * p + i
                            dst = area3[p % 3][:, i, :]
                            pe.matmul(dst[:, 0:T], stackq[0:ROWS, u, hd, P:T], stackk[0:ROWS, u, hd, :],
                                      start=True, stop=False)
                            pe.matmul(dst[:, P:T], identb[:], causal[:], start=False, stop=True)
                            pe.matmul(dst[:, T:T + P], stackq[0:ROWS, u, hd, 0:P], stackk[0:ROWS, u, hd, 0:P],
                                      start=True, stop=False)
                            mm = pe.matmul(dst[:, T:T + P], identb[:], causal[:], start=False, stop=True)
                        mm.then_inc(S["sn_mm"], 1)

                def shifted_scores(b, u, p):
                    if p < 2:
                        pe.wait_ge(S["mx_done"], PAIRS * b + 7 + p)
                    else:
                        pe.wait_ge(S["exp_done"], PAIRS * b + p - 1)
                    for i in range(2):
                        hd = 2 * p + i
                        dst = area[p % 2][:, i, :]
                        pe.matmul(dst[:, 0:T], stackk[0:ROWS + 1, u, hd, 0:P], stackq[0:ROWS + 1, u, hd, :],
                                  start=True, stop=True)
                        mm = pe.matmul(dst[:, T:T + P], stackk[0:ROWS + 1, u, hd, P:T], stackq[0:ROWS + 1, u, hd, P:T],
                                       start=True, stop=True)
                    mm.then_inc(S["st_mm"], 1)

                def weigh_values(b, u, g):
                    pe.wait_ge(S["caus_done"], PAIRS * b + 2 * g + 2)
                    if g == 0:
                        upto(pe, "v_done", b + 1)
                        wait(pe, S["on_done"], QT * b)
                    if g == 2:
                        wait(pe, S["oT_done"], b)
                    for kt in range(QT):
                        for i in range(4):
                            pr = probs[:, 2 * g + i // 2, i % 2]
                            dst = pv_out[32 * i:32 * i + 32, g]
                            mm = pe.matmul(dst if kt == 0 else dst[:, P:T], vaug[:, u, kt, 4 * g + i, :],
                                           pr[:, 0:T] if kt == 0 else pr[:, T:T + P], start=(kt == 0), stop=(kt == 1))
                    mm.then_inc(S["pv_mm"], 1)

                def iteration(b, u, k):
                    if stages(b + 1, 0, LAST):
                        pe.wait_ge(S["xh_done"], QT * (b + 2))
                        wait(pe, S["h1_done"], b - 1)
                        turn(misc[1], lambda q, c: xh[:, q, c * P:(c + 1) * P], S["xT_mm"])
                    if stages(b, 0, LAST):
                        scores_for_max(b, u)
                    if stages(b - 2, 0, LAST):
                        pe.wait_ge(S["xn_done"], QT * (b - 1))
                        wait(pe, S["xslot_done"], b - 1)
                        upto(pe, "h0_done", b + 1)
                        turn(misc[0], lambda q, c: x2h[:, u, q, c * P:(c + 1) * P], S["xt2_mm"])
                    if stages(b - 1, 0, LAST):
                        pe.wait_ge(S["oa_done"], b)
                        if stages(b, 0, LAST):
                            pe.wait_ge(S["mx_done"], PAIRS * b + 6)
                        for q in range(QT):
                            for g in range(4):
                                mm = pe.transpose(turned[:, q, g * P:(g + 1) * P], oa[:, g, q * P:(q + 1) * P], ident[:])
                        mm.then_inc(S["ot1_mm"], 1)
                    if stages(b, 0, LAST):
                        pe.wait_ge(S["mneg_done"], 2 * (b + 1))
                        wait(pe, S["xt2_done"], b - 1)
                        for q in range(QT):
                            mm = pe.transpose(misc[0].bitcast(BF16)[0:HEADS, q * P:(q + 1) * P], mneg[:, q, :], identb[:])
                        mm.then_inc(S["mT_mm"], 1)
                    if stages(b - 2, 0, LAST):
                        pe.wait_ge(S["xt2_done"], b - 1)
                        upto(pe, "xT_done", b + 1)
                        for q in range(QT):
                            for c in range(DC):
                                mm = pe.matmul(misc[1][:, q * EXPERTS:(q + 1) * EXPERTS], x2T[:, c, q * P:(q + 1) * P],
                                               gate_wT[:, c, :], start=(c == 0), stop=(c == DC - 1))
                        mm.then_inc(S["lg_mm"], 1)
                    if stages(b + 1, 0, LAST):
                        pe.wait_ge(S["xT_done"], b + 2)
                        wait(pe, S["mT_done"], b + 1)
                        project_rows(misc[0], 0, S["q_mm"])
                        wait(pe, S["gl_done"], b - 1)
                        project_rows(misc[1], 1, S["k_mm"])
                        wait(pe, S["on_done"], QT * b)
                        project_tokens(turned[:, 0, :], xT, lambda c: w0T[:, 2, c, :], S["v_mm"])
                    if stages(b - 1, 0, LAST):
                        pe.wait_ge(S["on_done"], QT * b)
                        turn(turned[:, 1, :], lambda q, c: onat[:, q, c * P:(c + 1) * P], S["ot2_mm"])
                    if stages(b, 0, LAST):
                        pe.wait_ge(S["mrow"], 16 * (b + 1))
                        shifted_scores(b, u, 0)
                        shifted_scores(b, u, 1)
                    if stages(b + 2, 0, LAST):
                        pe.wait_ge(S["ew_done"], b + 3)
                        upto(pe, "qr_done", b + 1)
                        for q in range(QT):
                            mm = pe.matmul(misc[0][:, q * D:(q + 1) * D], ew[:, q * P:(q + 1) * P], tok_wT[:],
                                           start=True, stop=True)
                        mm.then_inc(S["tok_mm"], 1)
                    for g in range(5):
                        if g < 3 and stages(b, 0, LAST):
                            shifted_scores(b, u, 2 * g + 2)
                            shifted_scores(b, u, 2 * g + 3)
                        if g == 1 and stages(b - 1, 0, LAST):
                            pe.wait_ge(S["oT_done"], b)
                            upto(pe, "kr_done", b + 1)
                            project_tokens(misc[1], oT, lambda c: w0T[:, 3, c, :], S["wo_mm"])
                        if g == 3 and stages(b - 2, 0, LAST):
                            pe.wait_ge(S["hsum_done"], b - 1)
                            upto(pe, "h0_done", b + 2)
                            E = EXPERTS
                            pe.matmul(misc[0][:, 0:E], before[:], hsum[:, 0, :], start=True, stop=True)
                            pe.matmul(misc[0][:, E:2 * E], before[:], hsum[:, 1, :], start=True, stop=False)
                            pe.matmul(misc[0][:, E:2 * E], onesb[:], hsum[:, 0, :], start=False, stop=True)
                            pe.matmul(misc[0][:, 2 * E:3 * E], onesb[:], hsum[:, 0, :], start=True, stop=False)
                            mm = pe.matmul(misc[0][:, 2 * E:3 * E], onesb[:], hsum[:, 1, :], start=False, stop=True)
                            mm.then_inc(S["rk_mm"], 1)
                        if g >= 1 and stages(b, 0, LAST):
                            weigh_values(b, u, g - 1)

                batches(pe, iteration)

        def moe_tiles(eng, iteration):
            for i in range(-3, 2):
                iteration(i, i % 2, i // 2)
            with eng.Fori(0, (MOE_TILES - 5) // 2) as it:
                for u in range(2):
                    iteration(it * 2 + (2 + u), u, it + 1)
            for i in range(MOE_TILES - 3, MOE_TILES):
                iteration(i, i % 2, i // 2)

        def has(i):
            return not isinstance(i, int) or 0 <= i < MOE_TILES

        def expert_of(eng, i):
            return eng.value_load(tile_e[0:1, one(i)], min_val=0, max_val=EXPERTS - 1)

        with nc.Block() as block:
            @block.sync
            def _(sp):
                sp.dma_start(b2r, a["L0_ffn_b2"].rearrange("(o e) d -> o e d", o=1).to_broadcast([P, EXPERTS, D])).then_inc(S["b_in"], 16)
                sp.wait_ge(S["set_done"], 1)
                for e in range(EXPERTS):
                    n = sp.value_load(cnt[0:1, e:e + 1], min_val=0, max_val=TOKENS)
                    sp.dma_start(xg[bass.ds(n + e * CAP, P), :], zeros).then_inc(S["zfill"], 16)
                sp.wait_ge(S["zfill"], 16 * EXPERTS)

                def iteration(i, u, k):
                    v = 1 - u
                    if has(i + 3):
                        r = sp.value_load(tile_row[0:1, one(i + 3)], min_val=0, max_val=EXPERTS * CAP - P)
                        wait(sp, S["tx_mm"], i + 2)
                        sp.dma_start(xt_in[:, v], xg[bass.ds(r, P), :]).then_inc(x_ld[v], 16)
                    if has(i):
                        sp.wait_ge(S["y_ev"], i + 1)
                        sp.dma_start(yg[bass.ds(i * P, P), :], yt[:, u]).then_inc(y_st[u], 16)

                moe_tiles(sp, iteration)
                for u in range(2):
                    sp.wait_ge(y_st[u], 16 * ((MOE_TILES + 1 - u) // 2))

            @block.gpsimd
            def _(pool):
                pool.memset(zeros, 0.0).then_inc(S["set_done"], 1)
                pool.dma_start(b1raw[0:EXPERTS, :], a["L0_ffn_b1"]).then_inc(S["w_late"], 16)
                for e in range(EARLY, EXPERTS):
                    pool.wait_ge(S["w_late"], 16 + 32 * (e - EARLY))
                    pool.dma_start(w1s[:, e], a["L0_ffn_w1"][e].rearrange("(c p) n -> p c n", p=P)).then_inc(S["w_late"], 16)
                    pool.dma_start(w2s[:, e], a["L0_ffn_w2"][e].rearrange("(c p) n -> p c n", p=P)).then_inc(S["w_late"], 16)
                pool.wait_ge(S["w_late"], 16 + 32 * (EXPERTS - EARLY))

            def relu(eng, i, u, c):
                src = psum[:, 2 + c // 4, (c % 4) * P:(c % 4 + 1) * P]
                bias = b1c[:, u, c:c + 1]
                if eng is nc.scalar:
                    return eng.activation(hidT[:, u, c, :], src, ACT.Relu, bias=bias)
                return eng.tensor_scalar(hidT[:, u, c, :], src, bias, 0.0, ALU.add, ALU.max)

            @block.scalar
            def _(act):
                def iteration(i, u, k):
                    if has(i):
                        act.wait_ge(S["bias_done"], i + 1)
                        act.wait_ge(S["th_mm"], i + 1)
                        wait(act, S["l2_mm"], i - 1)
                        for c in range(HC // 2):
                            ins = relu(act, i, u, c)
                        ins.then_inc(S["reluA"], 1)
                    if has(i + 1):
                        act.wait_ge(S["l1_mm"], i + 2)
                        wait(act, S["th_mm"], i + 1)
                        act.copy(hid[:, 0:512], psum[:, 0, :]).then_inc(S["hidA"], 1)
                    if has(i + 2):
                        act.wait_ge(S["tx_mm"], i + 3)
                        wait(act, S["l1_mm"], i + 1)
                        act.copy(xtT[:, u].rearrange("p c t -> p (c t)"), misc[u][:, 0:D]).then_inc(S["xtT_done"], 1)

                moe_tiles(act, iteration)

            @block.vector
            def _(dve):
                dve.wait_ge(S["b1_mm"], 1)
                dve.tensor_copy(b1T.rearrange("p c e -> p (c e)"), misc[0][:, 0:HC * EXPERTS]).then_inc(S["b1_done"], 1)
                dve.wait_ge(S["b1_done"], 1)

                def iteration(i, u, k):
                    if has(i):
                        e = expert_of(dve, i)
                        wait(dve, S["reluA"], i - 1)
                        dve.tensor_copy(b1c[:, u, :], b1T[:, :, one(e)].rearrange("p c o -> p (c o)")).then_inc(S["bias_done"], 1)
                        dve.wait_ge(S["bias_done"], i + 1)
                        dve.wait_ge(S["th_mm"], i + 1)
                        wait(dve, S["l2_mm"], i - 1)
                        for c in range(HC // 2, HC):
                            ins = relu(dve, i, u, c)
                        ins.then_inc(S["reluD"], 1)
                    if has(i + 1):
                        dve.wait_ge(S["l1_mm"], i + 2)
                        wait(dve, S["th_mm"], i + 1)
                        dve.tensor_copy(hid[:, 512:1024], psum[:, 1, :]).then_inc(S["hidD"], 1)
                    if has(i):
                        dve.wait_ge(S["l2_mm"], i + 1)
                        wait(dve, y_st[u], 16 * k)
                        dve.tensor_tensor(yt[:, u], psum[:, 4 + u, 0:D], b2r[:, one(e), :].rearrange("p o d -> p (o d)"),
                                          ALU.add).then_inc(S["y_ev"], 1)

                moe_tiles(dve, iteration)

            @block.tensor
            def _(pe):
                pe.wait_ge(S["b_in"], 16)
                pe.wait_ge(S["w_late"], 16)
                pe.wait_ge(S["w_exp"], 32 * EARLY)
                for c in range(HC):
                    mm = pe.transpose(misc[0][:, c * EXPERTS:(c + 1) * EXPERTS], b1raw[0:EXPERTS, c * P:(c + 1) * P],
                                      ident[0:EXPERTS, 0:EXPERTS])
                mm.then_inc(S["b1_mm"], 1)
                pe.wait_ge(S["b1_done"], 1)

                def iteration(i, u, k):
                    v = 1 - u
                    if has(i):
                        pe.wait_ge(S["hidA"], i + 1)
                        pe.wait_ge(S["hidD"], i + 1)
                        wait(pe, S["reluA"], i)
                        wait(pe, S["reluD"], i)
                        for c in range(HC):
                            mm = pe.transpose(psum[:, 2 + c // 4, (c % 4) * P:(c % 4 + 1) * P], hid[:, c * P:(c + 1) * P],
                                              ident[:])
                        mm.then_inc(S["th_mm"], 1)
                    if has(i + 1):
                        e = expert_of(pe, i + 1)
                        pe.wait_ge(S["w_late"], pe.value_load(tile_w[0:1, one(i + 1)], min_val=16, max_val=32 * EXPERTS))
                        pe.wait_ge(S["xtT_done"], i + 2)
                        for n in range(2):
                            for c in range(DC):
                                mm = pe.matmul(psum[:, n, :], xtT[:, v, c, :],
                                               w1s[:, one(e), c, n * 512:(n + 1) * 512].rearrange("p o n -> p (o n)"),
                                               start=(c == 0), stop=(c == DC - 1))
                        mm.then_inc(S["l1_mm"], 1)
                    if has(i + 2):
                        pe.wait_ge(x_ld[u], 16 * (k + 2))
                        wait(pe, S["xtT_done"], i + 1)
                        for c in range(DC):
                            mm = pe.transpose(misc[u][:, c * P:(c + 1) * P], xt_in[:, u, c * P:(c + 1) * P], ident[:])
                        mm.then_inc(S["tx_mm"], 1)
                    if has(i):
                        e = expert_of(pe, i)
                        pe.wait_ge(S["reluA"], i + 1)
                        pe.wait_ge(S["reluD"], i + 1)
                        wait(pe, S["y_ev"], i - 1)
                        for c in range(HC):
                            mm = pe.matmul(psum[:, 4 + u, 0:D], hidT[:, u, c, :],
                                           w2s[:, one(e), c, :].rearrange("p o n -> p (o n)"), start=(c == 0), stop=(c == HC - 1))
                        mm.then_inc(S["l2_mm"], 1)

                moe_tiles(pe, iteration)

        POOL_PAIRS = (0, 3)

        def products_made(eng, b, p, only=None):
            if p < 0:
                b, p = b - 1, p + PAIRS
            if p in POOL_PAIRS:
                wait(eng, S["prodP"], len(POOL_PAIRS) * b + POOL_PAIRS.index(p) + 1)
            else:
                mine = [x for x in range(PAIRS) if x not in POOL_PAIRS]
                wait(eng, S["prodD"], len(mine) * b + mine.index(p) + 1)

        with nc.Block() as block:
            @block.sync
            def _(sp):
                def bounce(b, u, which, done, landed_w):
                    sp.wait_ge(done, b + 1)
                    settled(sp)
                    wait(sp, S["s2_mm"], PAIRS * (b - 1))
                    sp.dma_start(scr[u, which].rearrange("s (j p) t -> p (s j) t", p=P),
                                 n_qkp[which].rearrange("p s j t -> p (s j) t")).then_inc(landed_w, 16)

                def gather(b, u, which, landed_w, landed_r, stack):
                    sp.wait_ge(landed_w, 16 * (b + 1))
                    for i, part in enumerate((Q_PARTS, K_PARTS)[which]):
                        sp.dma_start(stack[DH * i:DH * (i + 1), u],
                                     scr[u, which, part].rearrange("(h d) t -> d h t", d=DH)).then_inc(landed_r, 16)

                def iteration(b, u, k):
                    if stages(b + 1, 0, LAST):
                        bounce(b + 1, 1 - u, 0, S["n_ql"], S["n_scrq"])
                        bounce(b + 1, 1 - u, 1, S["n_kl"], S["n_scrk"])
                        gather(b + 1, 1 - u, 0, S["n_scrq"], S["n_stkq"], stackq1)
                        gather(b + 1, 1 - u, 1, S["n_scrk"], S["n_stkk"], stackk1)

                batches(sp, iteration)

            @block.gpsimd
            def _(pool):
                def norm_scale(b, n, got, s_eps, s_rstd):
                    pool.wait_ge(got, QT * (b + 1))
                    settled(pool)
                    scale, shift = (1.0 + LN1_EPS, LN_EPS * LN1_EPS) if n == 0 else (1.0, LN_EPS)
                    pool.tensor_scalar(n_veps[:, n, :], n_mom[:, n, :, 1], scale, shift, ALU.mult, ALU.add).then_inc(s_eps, 1)
                    pool.wait_ge(s_eps, b + 1)
                    pool.tensor_tensor(n_rs[:, n, :], n_veps[:, n, :], half_exp[:], ALU.pow).then_inc(s_rstd, 1)

                def multiply(b, u, p):
                    pool.wait_ge(S["f2_done"], PAIRS * b + p + 1)
                    pool.tensor_tensor(first[:, u, p], first[:, u, p], second[:, p % 4], ALU.mult).then_inc(S["prodP"], 1)

                def iteration(b, u, k):
                    if stages(b + 2, 0, LAST):
                        pool.wait_ge(S["ypos_done"], 2 * (b + 3))
                        wait(pool, S["comb_done"], 4 * (b + 2))
                        settled(pool)
                        for c in range(TOPK):
                            for q in range(QT):
                                pool.indirect_dma_start(
                                    out=n_y[:, c, q, :], out_offset=None, in_=yg,
                                    in_offset=bass.IndirectOffsetOnAxis(ap=ypos[:, c, q:q + 1], axis=0)).then_inc(y_in[u], 16)
                    if stages(b - 1, 0, LAST):
                        pool.wait_ge(S["n_xh"], QT * b)
                        v = h[:, bass.ds((b - 1) * QT, QT), :]
                        pool.tensor_tensor(v, v, bo1[:].rearrange("p (o d) -> p o d", o=1).to_broadcast([P, QT, D]),
                                           ALU.add).then_inc(S["n_hbo"], 1)
                    if stages(b + 2, 0, LAST):
                        norm_scale(b + 2, 0, S["n_mv"], S["n_eps"], S["n_rstd"])
                    if stages(b - 1, 0, LAST):
                        norm_scale(b - 1, 1, S["m_mv"], S["m_eps"], S["m_rstd"])
                    if stages(b, 0, LAST):
                        for p in POOL_PAIRS:
                            multiply(b, u, p)

                batches(pool, iteration)

            @block.scalar
            def _(act):
                FIRST = (ACT.Exp, ACT.Sigmoid)

                def function(out, in_, f):
                    if f == ACT.Exp:
                        return act.activation(out, in_, ACT.Exp)
                    return act.activation(out, in_, ACT.Sigmoid, bias=neg_mu[:])

                def iteration(b, u, k):
                    v = 1 - u

                    def pass1(p):
                        if stages(b, 0, LAST):
                            act.wait_ge(S["s1_mm"], PAIRS * b + p + 1)
                            function(first[:, u, p], area[p % 2], FIRST[u]).then_inc(S["f1_done"], 1)

                    def high(which, got, scr_w, done):
                        act.wait_ge(got, b + 2)
                        wait(act, scr_w, 16 * (b + 1))
                        for j in range(DC):
                            ins = act.activation(n_qkp[which][:, 0, j], misc[which][:, j * T:(j + 1) * T], ACT.Identity,
                                                 bias=cols[:, 2 + which, j:j + 1])
                        ins.then_inc(done, 1)

                    def second_part(which, got, done):
                        act.wait_ge(got, b + 2)
                        act.copy(n_qkp[which][:, 1], n_qkr[which]).then_inc(done, 1)

                    pass1(0)
                    pass1(1)
                    if stages(b - 1, 0, LAST):
                        act.wait_ge(S["n_pv"], 4 * b)
                        wait(act, S["n_ot1"], b - 1)
                        act.copy(n_oa, pv_out).then_inc(S["n_oa"], 1)
                    pass1(2)
                    if stages(b + 1, 0, LAST):
                        act.wait_ge(S["n_xT_mm"], b + 2)
                        wait(act, S["n_v_mm"], b + 1)
                        for c in range(DC):
                            ins = act.activation(n_xT[:, c], misc[1][:, c * T:(c + 1) * T], ACT.Identity,
                                                 scale=cols[:, 0, c:c + 1], bias=cols[:, 1, c:c + 1])
                        ins.then_inc(S["n_xT_done"], 1)
                    pass1(3)
                    if stages(b + 1, 0, LAST):
                        high(0, S["n_q_mm"], S["n_scrq"], S["n_qh"])
                    pass1(4)
                    if stages(b + 1, 0, LAST):
                        high(1, S["n_k_mm"], S["n_scrk"], S["n_kh"])
                        second_part(0, S["n_qr"], S["n_qm"])
                    pass1(5)
                    if stages(b - 1, 0, LAST):
                        act.wait_ge(S["n_ot2"], b)
                        wait(act, S["n_wo"], b - 1)
                        act.copy(n_oT.rearrange("p c t -> p (c t)"), misc[0]).then_inc(S["n_oT"], 1)
                    if stages(b + 1, 0, LAST):
                        second_part(1, S["n_kr"], S["n_km"])
                    pass1(6)
                    pass1(7)
                    if stages(b, 0, LAST):
                        for p in range(PAIRS):
                            act.wait_ge(S["s2_mm"], PAIRS * b + p + 1)
                            products_made(act, b, p - 4)
                            function(second[:, p % 4], area[p % 2], FIRST[v]).then_inc(S["f2_done"], 1)

                batches(act, iteration)

            @block.vector
            def _(dve):
                dve.memset(n_vaug[:, :, :, :, DH:32], 1.0).then_inc(S["set_done"], 1)
                dve.memset(amax[:, 1], 0.0).then_inc(S["set_done"], 1)

                def statistics(b, n, s_stat, s_mv):
                    settled(dve)
                    for q in range(QT):
                        dve.bn_stats(n_bst[:, n, q, :], h[:, one(b * QT + q), :].rearrange("p o d -> p (o d)")).then_inc(s_stat, 1)
                    dve.wait_ge(s_stat, QT * (b + 1))
                    settled(dve)
                    for q in range(QT):
                        dve.bn_aggr(n_mom[:, n, q, :], n_bst[:, n, q, :]).then_inc(s_mv, 1)

                def split_rest(b, which, got, rest):
                    dve.wait_ge(got, b + 1)
                    for j in range(DC):
                        ins = dve.scalar_tensor_tensor(out=n_qkr[which][:, j], in0=misc[which][:, j * T:(j + 1) * T],
                                                       scalar=cols[:, 2 + which, j:j + 1], in1=n_qkp[which][:, 0, j],
                                                       op0=ALU.add, op1=ALU.subtract)
                    ins.then_inc(rest, 1)

                def split_last(b, which, second_part, last):
                    dve.wait_ge(second_part, b + 1)
                    dve.tensor_tensor(n_qkp[which][:, 2], n_qkr[which], n_qkp[which][:, 1], ALU.subtract).then_inc(last, 1)

                def multiply(b, u, p):
                    dve.wait_ge(S["f2_done"], PAIRS * b + p + 1)
                    dve.tensor_tensor(first[:, u, p], first[:, u, p], second[:, p % 4], ALU.mult).then_inc(S["prodD"], 1)

                def iteration(b, u, k):
                    v = 1 - u
                    if stages(b + 2, 0, LAST):
                        wait(dve, y_in[v], 64 * (parity_count(k, u, 1)))
                        dve.tensor_copy(ypos[:], pos[:, :, bass.ds((b + 2) * QT, QT)]).then_inc(S["ypos_done"], 1)
                        wait(dve, S["comb_done"], 4 * (b + 2))
                        dve.tensor_copy(n_gate, gates[:, bass.ds((b + 2) * QT, QT), :]).then_inc(S["ypos_done"], 1)
                    if stages(b - 1, 0, LAST):
                        dve.wait_ge(S["n_ot1"], b)
                        wait(dve, S["n_on"], QT * (b - 1))
                        o1 = turned.rearrange("p q (h c) -> p q h c", c=32)
                        for q in range(QT):
                            dve.reciprocal(n_rr[:, q, :], o1[:, q, :, DH]).then_inc(S["n_rr"], 1)
                        for q in range(QT):
                            dve.wait_ge(S["n_rr"], QT * (b - 1) + q + 1)
                            wait(dve, S["n_ot2"], b - 1)
                            dve.tensor_tensor(n_onat[:, q].rearrange("p (h d) -> p h d", d=DH), o1[:, q, :, 0:DH],
                                              n_rr[:, q, :].rearrange("p (h o) -> p h o", o=1).to_broadcast([P, HEADS, DH]),
                                              ALU.mult).then_inc(S["n_on"], 1)
                    if stages(b + 1, 0, LAST):
                        wait(dve, S["n_qm"], b + 1)
                        split_rest(b + 1, 0, S["n_qh"], S["n_qr"])
                        split_rest(b + 1, 1, S["n_kh"], S["n_kr"])
                    if stages(b + 2, 0, LAST):
                        dve.wait_ge(y_in[u], 64 * (parity_count(k, u, 2)))
                        dve.wait_ge(S["ypos_done"], 2 * (b + 3))
                        for c in range(TOPK):
                            for q in range(QT):
                                hv = h[:, one((b + 2) * QT + q), :].rearrange("p o d -> p (o d)")
                                if c == 1:
                                    dve.wait_ge(S["comb_done"], 4 * (b + 2) + q + 1)
                                dve.scalar_tensor_tensor(out=hv, in0=n_y[:, c, q, :], scalar=n_gate[:, q, c:c + 1], in1=hv,
                                                         op0=ALU.mult, op1=ALU.add).then_inc(S["comb_done"], 1)
                        dve.wait_ge(S["comb_done"], 4 * (b + 3))
                        wait(dve, S["n_xh"], QT * (b + 2))
                        statistics(b + 2, 0, S["n_stat"], S["n_mv"])
                    if stages(b + 1, 0, LAST):
                        split_last(b + 1, 0, S["n_qm"], S["n_ql"])
                        dve.wait_ge(S["n_v_mm"], b + 2)
                        dve.tensor_tensor(n_vaug[:, v, :, :, 0:DH], misc[1].rearrange("p (q h d) -> p q h d", q=QT, h=HEADS),
                                          bv1[:].rearrange("p (o h d) -> p o h d", o=1, h=HEADS).to_broadcast([P, QT, HEADS, DH]),
                                          ALU.add).then_inc(S["n_v_done"], 1)
                        split_last(b + 1, 1, S["n_km"], S["n_kl"])
                    if stages(b - 1, 0, LAST):
                        dve.wait_ge(S["n_wo"], b)
                        dve.wait_ge(S["n_hbo"], b)
                        hv = h[:, bass.ds((b - 1) * QT, QT), :]
                        dve.tensor_tensor(hv, misc[0].rearrange("p (q d) -> p q d", q=QT), hv, ALU.add).then_inc(S["n_h3"], 1)
                        dve.wait_ge(S["n_h3"], b)
                        wait(dve, S["x3_done"], QT * (b - 1))
                        statistics(b - 1, 1, S["m_stat"], S["m_mv"])
                    if stages(b + 2, 0, LAST):
                        wait(dve, S["n_xT_mm"], b + 2)
                        dve.wait_ge(S["n_rstd"], b + 3)
                        for q in range(QT):
                            dve.tensor_scalar(n_xh[:, q:q + 1, :], h[:, one((b + 2) * QT + q), :], n_mom[:, 0, q, 0:1],
                                              n_rs[:, 0, q:q + 1], ALU.subtract, ALU.mult).then_inc(S["n_xh"], 1)
                    for p in range(PAIRS):
                        if p not in POOL_PAIRS and stages(b, 0, LAST):
                            multiply(b, u, p)
                    if stages(b - 1, 0, LAST):
                        dve.wait_ge(S["m_rstd"], b)
                        for q in range(QT):
                            dve.tensor_scalar(x3[:, one((b - 1) * QT + q), :], h[:, one((b - 1) * QT + q), :],
                                              n_mom[:, 1, q, 0:1], n_rs[:, 1, q:q + 1], ALU.subtract,
                                              ALU.mult).then_inc(S["x3_done"], 1)
                        dve.wait_ge(S["x3_done"], QT * b)
                        wait(dve, S["am_done"], 2 * (b - 1))
                        settled(dve)
                        dve.tensor_reduce(amax[:, 0], x3[:, bass.ds((b - 1) * QT, QT), :], AX, ALU.max,
                                          apply_absolute_value=True).then_inc(S["am_done"], 1)
                        dve.wait_ge(S["am_done"], 2 * b - 1)
                        dve.tensor_tensor(amax[:, 1], amax[:, 1], amax[:, 0], ALU.max).then_inc(S["am_done"], 1)

                batches(dve, iteration)

            @block.tensor
            def _(pe):
                pe.wait_ge(S["set_done"], 3)

                def turn(bank, src, done):
                    for c in range(DC):
                        for q in range(QT):
                            mm = pe.transpose(bank[:, c * T + q * P:c * T + (q + 1) * P], src(q, c), ident[:])
                    mm.then_inc(done, 1)

                def project_rows(bank, w, done):
                    for j in range(DC):
                        for c in range(DC):
                            mm = pe.matmul(bank[:, j * T:(j + 1) * T], w1T[:, w, c, j * P:(j + 1) * P], n_xT[:, c, :],
                                           start=(c == 0), stop=(c == DC - 1))
                    mm.then_inc(done, 1)

                def project_tokens(bank, x, w, done):
                    for q in range(QT):
                        for c in range(DC):
                            mm = pe.matmul(bank[:, q * D:(q + 1) * D], x[:, c, q * P:(q + 1) * P], w1T[:, w, c, :],
                                           start=(c == 0), stop=(c == DC - 1))
                    mm.then_inc(done, 1)

                def scores(b, u, p, done):
                    for i in range(2):
                        hd = 2 * p + i
                        for kt in range(QT):
                            mm = pe.matmul(area[p % 2][:, i, kt * T:(kt + 1) * T],
                                           stackk1[0:ROWS, u, hd, kt * P:(kt + 1) * P], stackq1[0:ROWS, u, hd, :],
                                           start=True, stop=True)
                    mm.then_inc(done, 1)

                def weigh_values(b, u, g):
                    products_made(pe, b, 2 * g)
                    products_made(pe, b, 2 * g + 1)
                    if g == 0:
                        pe.wait_ge(S["n_v_done"], b + 1)
                        wait(pe, S["n_on"], QT * b)
                    for kt in range(QT):
                        for i in range(4):
                            mm = pe.matmul(pv_out[32 * i:32 * i + 32, g], n_vaug[:, u, kt, 4 * g + i, :],
                                           first[:, u, 2 * g + i // 2, i % 2, kt * T:(kt + 1) * T],
                                           start=(kt == 0), stop=(kt == QT - 1))
                    mm.then_inc(S["n_pv"], 1)

                def iteration(b, u, k):
                    v = 1 - u

                    def pass1(p):
                        if stages(b, 0, LAST):
                            if p == 0:
                                pe.wait_ge(S["n_stkq"], 16 * SLOTS6 * (b + 1))
                                pe.wait_ge(S["n_stkk"], 16 * SLOTS6 * (b + 1))
                            if p < 2:
                                wait(pe, S["f2_done"], PAIRS * b - 1 + p)
                            else:
                                pe.wait_ge(S["f1_done"], PAIRS * b + p - 1)
                            scores(b, u, p, S["s1_mm"])

                    pass1(0)
                    pass1(1)
                    if stages(b - 1, 0, LAST):
                        weigh_values(b - 1, v, 2)
                        weigh_values(b - 1, v, 3)
                    pass1(2)
                    if stages(b + 1, 0, LAST):
                        pe.wait_ge(S["n_xh"], QT * (b + 2))
                        wait(pe, S["n_v_done"], b + 1)
                        turn(misc[1], lambda q, c: n_xh[:, q, c * P:(c + 1) * P], S["n_xT_mm"])
                    pass1(3)
                    if stages(b - 1, 0, LAST):
                        pe.wait_ge(S["n_oa"], b)
                        for q in range(QT):
                            for g in range(4):
                                mm = pe.transpose(turned[:, q, g * P:(g + 1) * P], n_oa[:, g, q * P:(q + 1) * P], ident[:])
                        mm.then_inc(S["n_ot1"], 1)
                    if stages(b + 1, 0, LAST):
                        pe.wait_ge(S["n_xT_done"], b + 2)
                        wait(pe, S["n_h3"], b - 1)
                        project_rows(misc[0], 0, S["n_q_mm"])
                    pass1(4)
                    if stages(b + 1, 0, LAST):
                        project_rows(misc[1], 1, S["n_k_mm"])
                    pass1(5)
                    if stages(b - 1, 0, LAST):
                        pe.wait_ge(S["n_on"], QT * b)
                        upto(pe, "n_qr", b + 1)
                        turn(misc[0], lambda q, c: n_onat[:, q, c * P:(c + 1) * P], S["n_ot2"])
                    pass1(6)
                    if stages(b + 1, 0, LAST):
                        pe.wait_ge(S["n_kr"], b + 2)
                        project_tokens(misc[1], n_xT, 2, S["n_v_mm"])
                    pass1(7)
                    if stages(b - 1, 0, LAST):
                        pe.wait_ge(S["n_oT"], b)
                        project_tokens(misc[0], n_oT, 3, S["n_wo"])
                    if stages(b, 0, LAST):
                        for p in range(PAIRS):
                            if p < 2:
                                pe.wait_ge(S["f1_done"], PAIRS * b + 7 + p)
                            else:
                                pe.wait_ge(S["f2_done"], PAIRS * b + p - 1)
                            scores(b, u, p, S["s2_mm"])
                            if p in (5, 7):
                                weigh_values(b, u, (p - 5) // 2)

                batches(pe, iteration)

        EXPONENT = 0x7F800000
        ROUNDER = 1.5 * 2.0 ** 20

        with nc.Block() as block:
            @block.sync
            def _(sp):
                sp.dma_start(w8, a["L1_ffn_weight"].rearrange("(j p) i -> p j i", p=P)).then_inc(S["w8_in"], 16)
                for b in range(B):
                    sp.wait_ge(S["f_out"], b + 1)
                    sp.dma_start(out[b].rearrange("(q p) d -> p q d", p=P), f_out[:, b % 2]).then_inc(o_out[b % 2], 16)
                for u in range(2):
                    sp.wait_ge(o_out[u], 16 * B // 2)

            @block.scalar
            def _(act):
                for n in range(B + 1):
                    act.wait_ge(S["fT_mm"], n + 1)
                    if n >= 3:
                        act.wait_ge(S["f_mm"], n - 2)
                    dst = fqT[:] if n == 0 else f_qT[:, n % 2]
                    act.copy(dst.rearrange("p c t -> p (c t)"), psum[:, 2 + n % 2, 0:T].bitcast(BF16)).then_inc(S["fT_done"], 1)

            @block.vector
            def _(dve):
                steps = [0]

                def chain(ins):
                    steps[0] += 1
                    ins.then_inc(S["q_step"], 1)
                    dve.wait_ge(S["q_step"], steps[0])

                dve.wait_ge(S["w8_in"], 16)
                chain(dve.tensor_reduce(amaxes[:, 0:1], w8.rearrange("p c d -> p (c d)"), AX, ALU.max,
                                        apply_absolute_value=True))
                dve.tensor_reduce(amaxes[:, 1:2], amax[:, 1], AX, ALU.max).then_inc(S["am_done"], 1)
                dve.wait_ge(S["am_mm"], 1)
                chain(dve.tensor_reduce(amax_r[0:1], psum[0:1, 0, 0:2 * P].rearrange("o (n p) -> o n p", n=2), AX, ALU.max))
                chain(dve.tensor_scalar(amax_r[0:1], amax_r[0:1], 1e-12, None, ALU.max))
                chain(dve.reciprocal(amax_r[0:1], amax_r[0:1]))
                chain(dve.tensor_scalar(scale_r[0:1, 0:2], amax_r[0:1], FP8_MAX, FP8_MAX, ALU.mult, ALU.min))
                chain(dve.reciprocal(amax_r[0:1], scale_r[0:1, 0:2]))
                chain(dve.tensor_tensor(scale_r[0:1, 2:3], amax_r[0:1, 0:1], amax_r[0:1, 1:2], ALU.mult))
                dve.tensor_copy(scale_r[0:1, 3:4], scale_r[0:1, 2:3]).then_inc(S["am_row"], 1)
                dve.wait_ge(S["sc_mm"], 1)
                chain(dve.tensor_copy(scales, psum[:, 0, 0:4]))

                def quantise(n):
                    u = n % 2
                    x = w8 if n == 0 else x3[:, (n - 1) * QT:n * QT, :]
                    y, e, t, q = f_y[:, u], f_e[:, u], f_t[:, u], f_q[:, u]
                    s = scales[:, 0:1] if n == 0 else scales[:, 1:2]
                    chain(dve.tensor_scalar(y, x, s, FP8_MAX, ALU.mult, ALU.min))
                    chain(dve.tensor_single_scalar(e, y.bitcast(I32), EXPONENT, op=ALU.bitwise_and))
                    chain(dve.tensor_scalar(e.bitcast(F32), e.bitcast(F32), 2.0 ** -6, ROUNDER, ALU.max, ALU.mult))
                    chain(dve.scalar_tensor_tensor(out=t, in0=y, scalar=-FP8_MAX, in1=e.bitcast(F32), op0=ALU.max, op1=ALU.add))
                    if n >= 2:
                        dve.wait_ge(S["fT_mm"], n - 1)
                    dve.tensor_tensor(q, t, e.bitcast(F32), ALU.subtract).then_inc(S["qz_q"], 1)

                def finish(b):
                    u = b % 2
                    dve.wait_ge(S["f_mm"], b + 1)
                    o, r = f_o[:, u], f_out[:, u]
                    if b >= 2:
                        dve.wait_ge(o_out[u], 16 * (b // 2))
                    dve.scalar_tensor_tensor(out=o, in0=psum[:, 4 + u, :].rearrange("p (q d) -> p q d", q=QT), scalar=scales[:, 2:3],
                                             in1=ffn_b[:].rearrange("p (o d) -> p o d", o=1).to_broadcast([P, QT, D]),
                                             op0=ALU.mult, op1=ALU.add).then_inc(S["f_o"], 1)
                    dve.wait_ge(S["f_o"], b + 1)
                    dve.tensor_tensor(r, h[:, b * QT:(b + 1) * QT, :], o, ALU.add).then_inc(S["f_out"], 1)

                for n in range(B + 1):
                    quantise(n)
                    if n >= 2:
                        finish(n - 2)
                finish(B - 1)

            @block.tensor
            def _(pe):
                pe.wait_ge(S["q_step"], 1)
                pe.wait_ge(S["am_done"], 2 * B + 1)
                for i in range(2):
                    mm = pe.transpose(psum[0:1, 0, i * P:(i + 1) * P], amaxes[:, i:i + 1], ident[:])
                mm.then_inc(S["am_mm"], 1)
                pe.wait_ge(S["am_row"], 1)
                pe.matmul(psum[:, 0, 0:4], ones_row[:], scale_r[0:1, :], start=True, stop=True).then_inc(S["sc_mm"], 1)
                for n in range(B + 1):
                    u = n % 2
                    pe.wait_ge(S["qz_q"], n + 1)
                    if n >= 2:
                        pe.wait_ge(S["fT_done"], n - 1)
                    for c in range(DC):
                        for q in range(QT):
                            mm = pe.transpose(psum[:, 2 + u, 0:T].bitcast(BF16)[:, c * T + q * P:c * T + (q + 1) * P],
                                              f_q[:, u, q, c * P:(c + 1) * P], identb[:])
                    mm.then_inc(S["fT_mm"], 1)
                    if n >= 1:
                        b = n - 1
                        pe.wait_ge(S["fT_done"], n + 1)
                        if b >= 2:
                            pe.wait_ge(S["f_o"], b - 1)
                        for q in range(QT):
                            for c in range(DC):
                                mm = pe.matmul(psum[:, 4 + b % 2, q * D:(q + 1) * D], f_qT[:, u, c, q * P:(q + 1) * P],
                                               fqT[:, c, :], start=(c == 0), stop=(c == DC - 1))
                        mm.then_inc(S["f_mm"], 1)


_INS = ["x", "L0_tok_W", "L0_tok_b", "L0_attn_Wq", "L0_attn_Wk", "L0_attn_Wv", "L0_attn_Wo", "L0_attn_bo",
        "L0_ffn_gate_w", "L0_ffn_gate_b", "L0_ffn_w1", "L0_ffn_b1", "L0_ffn_w2", "L0_ffn_b2",
        "L1_attn_ln_gamma", "L1_attn_ln_beta", "L1_attn_Wq", "L1_attn_bq", "L1_attn_Wk", "L1_attn_bk",
        "L1_attn_Wv", "L1_attn_bv", "L1_attn_Wo", "L1_attn_bo", "L1_attn_mu", "L1_ffn_weight", "L1_ffn_bias"]


def kernel(**inputs):
    import numpy as _np
    import concourse.bacc as _bacc
    from concourse import mybir as _mybir
    from concourse.bass_utils import run_bass_kernel_spmd as _run

    nc = _bacc.Bacc("TRN2", target_bir_lowering=False, num_devices=1)
    arrays, args = {}, {}
    for name in _INS:
        a = _np.ascontiguousarray(inputs[name])
        arrays[f"in_{name}_dram"] = a
        args[name] = nc.dram_tensor(f"in_{name}_dram", a.shape, _mybir.dt.from_np(a.dtype), kind="ExternalInput").ap()
    out = nc.dram_tensor("out_0_dram", (B, T, D), _mybir.dt.float32, kind="ExternalOutput").ap()
    tower_kernel(nc, args, out)
    r = _run(nc, [arrays], core_ids=[0])
    return r.results[0]["out_0_dram"]
```
